# Optimizing a Trainium2 kernel written in Bass

```python
import numpy as np
import jax
import jax.numpy as jnp

def _softmax(x, axis=-1):
    return jax.nn.softmax(x, axis=axis)

def _gelu(x):
    return jax.nn.gelu(x, approximate=True)

def _silu(x):
    return jax.nn.silu(x)

def _sigmoid(x):
    return jax.nn.sigmoid(x)

def _layernorm(x, axis=-1, eps=1e-05):
    m = jnp.mean(x, axis=axis, keepdims=True)
    v = jnp.var(x, axis=axis, keepdims=True)
    return (x - m) / jnp.sqrt(v + eps)

def _scatter_add(tgt, idx, src, axis=0):
    return tgt.at[idx].add(src)

def _segment_sum(src, seg, n):
    return jax.ops.segment_sum(src, seg, n)
kernel_name = 'mk_xattn_ffn_d1_seqx_r4_a02150'

def setup_inputs(seed: int=0):
    np.random.seed(seed)
    _w = jnp.asarray

    def _rec_inputs():
        import jax
        import jax.numpy as jnp
        _rk = jax.random.key(seed)
        x = -0.0002928 + 1 * jax.random.normal(jax.random.fold_in(_rk, 1), (8, 256, 256), jnp.float32)
        _lenS = 256 - jax.random.randint(jax.random.fold_in(_rk, 7), (8,), 0, max(1, 256 // 4) + 1, jnp.int32)
        _lenS2 = 256 - jax.random.randint(jax.random.fold_in(_rk, 8), (8,), 0, max(1, 256 // 4) + 1, jnp.int32)
        _ctx_1024P = jax.random.normal(jax.random.fold_in(_rk, 11), (8, 16, 256), jnp.float32)
        _ctx_1024c = jax.random.dirichlet(jax.random.fold_in(_rk, 511), 0.3 * jnp.ones((16,), jnp.float32), (8, 256))
        _ctx_1024t = jnp.einsum('bsk,bkd->bsd', _ctx_1024c, _ctx_1024P)
        _ctx_1024t = _ctx_1024t * jax.lax.rsqrt(jnp.mean(jnp.square(_ctx_1024t)) + 1e-12) * 0.953939
        ctx_1024 = -1.39393e-06 + 0.999914 * (_ctx_1024t + 0.3 * jax.random.normal(jax.random.fold_in(_rk, 611), (8, 256, 256), jnp.float32))
        _validS = jnp.arange(256)[None, :] < _lenS[:, None]
        _validS2 = jnp.arange(256)[None, :] < _lenS2[:, None]
        _causal = jnp.tril(jnp.ones((256, 256), dtype=bool))
        mask_BxS2_bk0 = jnp.logical_not(jnp.broadcast_to(_validS2[:, :], (8, 256)))
        return (x, ctx_1024, mask_BxS2_bk0)
    x, ctx_1024, mask_BxS2_bk0 = _rec_inputs()

    def _L0_xattn_setup():
        import jax, jax.numpy as jnp
        import numpy as np
        B, S, D = (2, 512, 256)
        H, DH = (16, 64)
        INNER = H * DH
        FF = 1024
        SCALE = DH ** (-0.5)
        EPS = 1e-05

        def layernorm(x, g, b):
            m = jnp.mean(x, axis=-1, keepdims=True)
            v = jnp.var(x, axis=-1, keepdims=True)
            return (x - m) * jax.lax.rsqrt(v + EPS) * g + b

        def attention(x, ctx, mask, wq, wk, wv, wo, bo):
            b, n, _ = x.shape
            j = ctx.shape[1]
            q = (x @ wq).reshape(b, n, H, DH).transpose(0, 2, 1, 3)
            k = (ctx @ wk).reshape(b, j, H, DH).transpose(0, 2, 1, 3)
            v = (ctx @ wv).reshape(b, j, H, DH).transpose(0, 2, 1, 3)
            sim = jnp.einsum('bhid,bhjd->bhij', q, k) * SCALE
            if mask is not None:
                neg = -jnp.finfo(sim.dtype).max
                sim = jnp.where(mask[:, None, None, :], neg, sim)
            attn = jax.nn.softmax(sim, axis=-1)
            out = jnp.einsum('bhij,bhjd->bhid', attn, v)
            out = out.transpose(0, 2, 1, 3).reshape(b, n, INNER)
            return out @ wo + bo
        key = jax.random.key(seed)
        ks = jax.random.split(key, 26)
        w = lambda k, shp, fan: (jax.random.normal(k, shp, jnp.float32) / np.sqrt(fan)).astype(jnp.float32)
        return {'x': jax.random.normal(ks[0], (B, S, D), jnp.float32), 'enc_output': jax.random.normal(ks[1], (B, S, D), jnp.float32), 'sa_wq': w(ks[2], (D, INNER), D), 'sa_wk': w(ks[3], (D, INNER), D), 'sa_wv': w(ks[4], (D, INNER), D), 'sa_wo': w(ks[5], (INNER, D), INNER), 'sa_bo': jnp.zeros((D,), jnp.float32), 'ca_wq': w(ks[6], (D, INNER), D), 'ca_wk': w(ks[7], (D, INNER), D), 'ca_wv': w(ks[8], (D, INNER), D), 'ca_wo': w(ks[9], (INNER, D), INNER), 'ca_bo': jnp.zeros((D,), jnp.float32), 'ln1_g': jnp.ones((D,), jnp.float32), 'ln1_b': jnp.zeros((D,), jnp.float32), 'ln2_g': jnp.ones((D,), jnp.float32), 'ln2_b': jnp.zeros((D,), jnp.float32), 'ln3_g': jnp.ones((D,), jnp.float32), 'ln3_b': jnp.zeros((D,), jnp.float32), 'fc1_w': w(ks[10], (D, FF), D), 'fc1_b': jnp.zeros((FF,), jnp.float32), 'fc2_w': w(ks[11], (FF, D), FF), 'fc2_b': jnp.zeros((D,), jnp.float32), 'tgt_mask': jax.random.bernoulli(ks[12], 0.1, (B, S)), 'src_mask': jax.random.bernoulli(ks[13], 0.1, (B, S))}
    _L0_xattn_all = _L0_xattn_setup()
    _L0_xattn_in = {k: v for k, v in _L0_xattn_all.items() if k in ('sa_wq', 'sa_wk', 'sa_wv', 'sa_wo', 'sa_bo', 'ca_wq', 'ca_wk', 'ca_wv', 'ca_wo', 'ca_bo', 'ln1_g', 'ln1_b', 'ln2_g', 'ln2_b', 'ln3_g', 'ln3_b', 'fc1_w', 'fc1_b', 'fc2_w', 'fc2_b')}
    del _L0_xattn_all

    def _L0_ffn_setup():
        import jax, jax.numpy as jnp
        import numpy as np
        HIDDEN = 256
        INTER = 1024
        N_EXPERTS = 8

        def geglu(x, w1, w2, w3):
            return jax.nn.gelu(x @ w1, approximate=False) * (x @ w2) @ w3
        key = jax.random.key(seed)
        ks = jax.random.split(key, 8)
        s = 0.02
        x = jax.random.normal(ks[0], (2, 512, HIDDEN), dtype=jnp.float32)
        w1s = jax.random.normal(ks[1], (HIDDEN, INTER), dtype=jnp.float32) * s
        w2s = jax.random.normal(ks[2], (HIDDEN, INTER), dtype=jnp.float32) * s
        w3s = jax.random.normal(ks[3], (INTER, HIDDEN), dtype=jnp.float32) * s
        W1 = jax.random.normal(ks[4], (N_EXPERTS, HIDDEN, INTER), dtype=jnp.float32) * s
        W2 = jax.random.normal(ks[5], (N_EXPERTS, HIDDEN, INTER), dtype=jnp.float32) * s
        W3 = jax.random.normal(ks[6], (N_EXPERTS, INTER, HIDDEN), dtype=jnp.float32) * s
        Wg = jax.random.normal(ks[7], (HIDDEN, N_EXPERTS), dtype=jnp.float32) * s
        return {'x': x, 'w1s': w1s, 'w2s': w2s, 'w3s': w3s, 'W1': W1, 'W2': W2, 'W3': W3, 'Wg': Wg}
    _L0_ffn_all = _L0_ffn_setup()
    _L0_ffn_in = {k: v for k, v in _L0_ffn_all.items() if k in ('w1s', 'w2s', 'w3s', 'W1', 'W2', 'W3', 'Wg')}
    del _L0_ffn_all
    return {'x': x, 'ctx_1024': ctx_1024, 'mask_BxS2_bk0': mask_BxS2_bk0, 'L0_xattn_sa_wq': _L0_xattn_in['sa_wq'], 'L0_xattn_sa_wk': _L0_xattn_in['sa_wk'], 'L0_xattn_sa_wv': _L0_xattn_in['sa_wv'], 'L0_xattn_sa_wo': _L0_xattn_in['sa_wo'], 'L0_xattn_sa_bo': _L0_xattn_in['sa_bo'], 'L0_xattn_ca_wq': _L0_xattn_in['ca_wq'], 'L0_xattn_ca_wk': _L0_xattn_in['ca_wk'], 'L0_xattn_ca_wv': _L0_xattn_in['ca_wv'], 'L0_xattn_ca_wo': _L0_xattn_in['ca_wo'], 'L0_xattn_ca_bo': _L0_xattn_in['ca_bo'], 'L0_xattn_ln1_g': _L0_xattn_in['ln1_g'], 'L0_xattn_ln1_b': _L0_xattn_in['ln1_b'], 'L0_xattn_ln2_g': _L0_xattn_in['ln2_g'], 'L0_xattn_ln2_b': _L0_xattn_in['ln2_b'], 'L0_xattn_ln3_g': _L0_xattn_in['ln3_g'], 'L0_xattn_ln3_b': _L0_xattn_in['ln3_b'], 'L0_xattn_fc1_w': _L0_xattn_in['fc1_w'], 'L0_xattn_fc1_b': _L0_xattn_in['fc1_b'], 'L0_xattn_fc2_w': _L0_xattn_in['fc2_w'], 'L0_xattn_fc2_b': _L0_xattn_in['fc2_b'], 'L0_ffn_w1s': _L0_ffn_in['w1s'], 'L0_ffn_w2s': _L0_ffn_in['w2s'], 'L0_ffn_w3s': _L0_ffn_in['w3s'], 'L0_ffn_W1': _L0_ffn_in['W1'], 'L0_ffn_W2': _L0_ffn_in['W2'], 'L0_ffn_W3': _L0_ffn_in['W3'], 'L0_ffn_Wg': _L0_ffn_in['Wg']}

def reference(x, ctx_1024, mask_BxS2_bk0, L0_xattn_sa_wq, L0_xattn_sa_wk, L0_xattn_sa_wv, L0_xattn_sa_wo, L0_xattn_sa_bo, L0_xattn_ca_wq, L0_xattn_ca_wk, L0_xattn_ca_wv, L0_xattn_ca_wo, L0_xattn_ca_bo, L0_xattn_ln1_g, L0_xattn_ln1_b, L0_xattn_ln2_g, L0_xattn_ln2_b, L0_xattn_ln3_g, L0_xattn_ln3_b, L0_xattn_fc1_w, L0_xattn_fc1_b, L0_xattn_fc2_w, L0_xattn_fc2_b, L0_ffn_w1s, L0_ffn_w2s, L0_ffn_w3s, L0_ffn_W1, L0_ffn_W2, L0_ffn_W3, L0_ffn_Wg):
    import jax
    import jax.numpy as jnp

    def _L0_xattn_ref(x, enc_output, sa_wq, sa_wk, sa_wv, sa_wo, sa_bo, ca_wq, ca_wk, ca_wv, ca_wo, ca_bo, ln1_g, ln1_b, ln2_g, ln2_b, ln3_g, ln3_b, fc1_w, fc1_b, fc2_w, fc2_b, tgt_mask, src_mask):
        import jax, jax.numpy as jnp
        import numpy as np
        B, S, D = (2, 512, 256)
        H, DH = (16, 64)
        INNER = H * DH
        FF = 1024
        SCALE = DH ** (-0.5)
        EPS = 1e-05

        def layernorm(x, g, b):
            m = jnp.mean(x, axis=-1, keepdims=True)
            v = jnp.var(x, axis=-1, keepdims=True)
            return (x - m) * jax.lax.rsqrt(v + EPS) * g + b

        def attention(x, ctx, mask, wq, wk, wv, wo, bo):
            b, n, _ = x.shape
            j = ctx.shape[1]
            q = (x @ wq).reshape(b, n, H, DH).transpose(0, 2, 1, 3)
            k = (ctx @ wk).reshape(b, j, H, DH).transpose(0, 2, 1, 3)
            v = (ctx @ wv).reshape(b, j, H, DH).transpose(0, 2, 1, 3)
            sim = jnp.einsum('bhid,bhjd->bhij', q, k) * SCALE
            if mask is not None:
                neg = -jnp.finfo(sim.dtype).max
                sim = jnp.where(mask[:, None, None, :], neg, sim)
            attn = jax.nn.softmax(sim, axis=-1)
            out = jnp.einsum('bhij,bhjd->bhid', attn, v)
            out = out.transpose(0, 2, 1, 3).reshape(b, n, INNER)
            return out @ wo + bo
        a = attention(x, x, tgt_mask, sa_wq, sa_wk, sa_wv, sa_wo, sa_bo)
        x = layernorm(x + a, ln1_g, ln1_b)
        a = attention(x, enc_output, src_mask, ca_wq, ca_wk, ca_wv, ca_wo, ca_bo)
        x = layernorm(x + a, ln2_g, ln2_b)
        h = jax.nn.gelu(x @ fc1_w + fc1_b, approximate=False)
        ff = h @ fc2_w + fc2_b
        x = layernorm(x + ff, ln3_g, ln3_b)
        return x

    def _L0_ffn_ref(x, w1s, w2s, w3s, W1, W2, W3, Wg):
        import jax, jax.numpy as jnp
        import numpy as np
        HIDDEN = 256
        INTER = 1024
        N_EXPERTS = 8

        def geglu(x, w1, w2, w3):
            return jax.nn.gelu(x @ w1, approximate=False) * (x @ w2) @ w3
        B, T, C = x.shape
        xf = x.reshape(-1, C)
        shared = geglu(xf, w1s, w2s, w3s)
        logits = xf @ Wg
        idx = jnp.argmax(logits, axis=-1)
        final = jnp.zeros_like(xf)
        for e in range(N_EXPERTS):
            y = geglu(xf, W1[e], W2[e], W3[e])
            final = final + jnp.where((idx == e)[:, None], y, 0.0)
        return (shared + final).reshape(B, T, C)
    x = x + _L0_xattn_ref(_layernorm(x, axis=-1), ctx_1024, L0_xattn_sa_wq, L0_xattn_sa_wk, L0_xattn_sa_wv, L0_xattn_sa_wo, L0_xattn_sa_bo, L0_xattn_ca_wq, L0_xattn_ca_wk, L0_xattn_ca_wv, L0_xattn_ca_wo, L0_xattn_ca_bo, L0_xattn_ln1_g, L0_xattn_ln1_b, L0_xattn_ln2_g, L0_xattn_ln2_b, L0_xattn_ln3_g, L0_xattn_ln3_b, L0_xattn_fc1_w, L0_xattn_fc1_b, L0_xattn_fc2_w, L0_xattn_fc2_b, mask_BxS2_bk0, mask_BxS2_bk0)
    x = x + _L0_ffn_ref(_layernorm(x, axis=-1), L0_ffn_w1s, L0_ffn_w2s, L0_ffn_w3s, L0_ffn_W1, L0_ffn_W2, L0_ffn_W3, L0_ffn_Wg)
    return x

_drawn_inputs = setup_inputs


def setup_inputs(seed=0):
    import zlib

    import numpy as np

    out = dict(_drawn_inputs(seed))
    spreads = {'L0_xattn_sa_bo': (0.0, 0.1),
     'L0_xattn_ca_bo': (0.0, 0.1),
     'L0_xattn_ln1_g': (1.0, 0.2),
     'L0_xattn_ln1_b': (0.0, 0.1),
     'L0_xattn_ln2_g': (1.0, 0.2),
     'L0_xattn_ln2_b': (0.0, 0.1),
     'L0_xattn_ln3_g': (1.0, 0.2),
     'L0_xattn_ln3_b': (0.0, 0.1),
     'L0_xattn_fc1_b': (0.0, 0.274),
     'L0_xattn_fc2_b': (0.0, 0.1)}
    factors = {'L0_ffn_w1s': 3.112,
     'L0_ffn_w2s': 3.044,
     'L0_ffn_w3s': 3.045,
     'L0_ffn_W1': 3.111,
     'L0_ffn_W2': 3.033,
     'L0_ffn_W3': 3.032,
     'L0_ffn_Wg': 3.232}
    for name, (base, spread) in spreads.items():
        noise = np.random.default_rng([zlib.crc32(name.encode()), seed]).standard_normal(out[name].shape)
        drawn = base * np.exp(spread * noise) if base else spread * noise
        out[name] = jnp.asarray(drawn.astype(out[name].dtype))
    for name, factor in factors.items():
        out[name] = (out[name] * factor).astype(out[name].dtype)
    return out
```

```python
from contextlib import ExitStack

import concourse.bass as bass
from concourse import mybir

F32 = mybir.dt.float32
F32R = mybir.dt.float32r
BF16 = mybir.dt.bfloat16
I32 = mybir.dt.int32
U8 = mybir.dt.uint8
ACT = mybir.ActivationFunctionType
ALU = mybir.AluOpType
AX = mybir.AxisListType

P = 128
B, S, D = 8, 256, 256
T = B * S
H, DH = 16, 64
INNER = H * DH
FF = 1024
E = 8
KC = D // P
ST = S // P
PAIRS = H // 2
GROUPS = 4
HG = H // GROUPS
FC = FF // P
EPS = 1e-5
SCALE = DH ** -0.5
MASKED = -(2.0 ** 126)
LOWEST = -3.0e38
SLOT = 256
SLOTS = T // SLOT + E - 1
TT = T // P


class Links:

    def __init__(self, eng, sem, per_turn=0, turn=0, before=0):
        self.eng, self.sem, self.per_turn, self.turn, self.before, self.n = eng, sem, per_turn, turn, before, 0

    def mark(self, ins):
        ins.then_inc(self.sem, 1)
        self.n += 1

    def join(self):
        self.eng.wait_ge(self.sem, self.turn * self.per_turn + (self.before + self.n))

    def __call__(self, ins):
        self.mark(ins)
        self.join()

    def close(self):
        assert self.n == self.per_turn, (self.n, self.per_turn)


def product(pe, out, stationary, moving, start, stop):
    (wh, wl), (mh, ml) = stationary, moving
    pe.matmul(out, wl, mh, start=start, stop=False, skip_group_check=True)
    pe.matmul(out, wh, ml, start=False, stop=False, skip_group_check=True)
    return pe.matmul(out, wh, mh, start=False, stop=stop, skip_group_check=True)


def make_identity(pool, ident, sem):
    pool.memset(ident, 0.0).then_inc(sem, 1)
    pool.wait_ge(sem, 1)
    pool.affine_select(out=ident, in_=ident, compare_op=ALU.not_equal, fill=1.0, base=0,
                       pattern=[[-1, P]], channel_multiplier=1).then_inc(sem, 1)


def layer_norm(dve, link, gate, x, out, work, squares, stat, veps_ready, rstd_ready, rstd_at, g=None, beta=None):
    n = x.shape[1]
    total, nmean, ssq, veps, rstd = (stat[:, k, 0:n] for k in range(5))
    link(dve.tensor_reduce(total, x, AX.X, ALU.add))
    link(dve.tensor_scalar(nmean, total, -1.0 / D, None, ALU.mult))
    for t in range(n):
        link.mark(dve.tensor_scalar(work[:, t, :], x[:, t, :], nmean[:, t:t + 1], None, ALU.add))
    for t in range(n):
        link.join()
        dve.sem_inc(gate, 1)
        link.mark(dve.tensor_tensor_reduce(squares[:, t, :], work[:, t, :], work[:, t, :], 1.0, 0.0,
                                           ALU.mult, ALU.add, ssq[:, t:t + 1]))
    link.join()
    dve.tensor_scalar(veps, ssq, 1.0 / D, EPS, ALU.mult, ALU.add).then_inc(veps_ready, 1)
    dve.wait_ge(rstd_ready, rstd_at)
    for t in range(n):
        if g is None:
            link.mark(dve.tensor_scalar(out[:, t, :], work[:, t, :], rstd[:, t:t + 1], None, ALU.mult))
        else:
            link.mark(dve.scalar_tensor_tensor(out=out[:, t, :], in0=work[:, t, :],
                                               scalar=rstd[:, t:t + 1], in1=g, op0=ALU.mult, op1=ALU.mult))
    if g is not None:
        link.join()
        for t in range(n):
            link.mark(dve.tensor_tensor(out[:, t, :], out[:, t, :], beta, ALU.add))
    link.join()


def norm_links(n, affine):
    return 2 + 3 * n + (n if affine else 0)


def load_weights(nc, weights, prefix):
    PIECE = 2048
    with ExitStack() as ctx:
        raw = [ctx.enter_context(nc.sbuf_tensor(f"{prefix}_raw{i}", [P, PIECE], F32)) for i in range(3)]
        landed = [ctx.enter_context(nc.semaphore(f"{prefix}_landed{i}")) for i in range(3)]
        hi_ready = ctx.enter_context(nc.semaphore(f"{prefix}_hi_ready"))
        lo_ready = ctx.enter_context(nc.semaphore(f"{prefix}_lo_ready"))
        pieces = []
        for w, (hi, lo) in weights:
            k, n = w.shape
            step = PIECE // n
            for c in range(0, k // P, step):
                pieces.append((w.rearrange("(c p) n -> p c n", p=P)[:, c:c + step, :], n,
                               hi[:, c * n:(c + step) * n], lo[:, c * n:(c + step) * n]))
        with nc.Block() as block:
            @block.sync
            def _(sp):
                for i, (src, n, _, _) in enumerate(pieces):
                    if i >= 3:
                        sp.wait_ge(lo_ready, i - 2)
                    sp.dma_start(raw[i % 3][:, :].rearrange("p (c n) -> p c n", n=n), src).then_inc(landed[i % 3], 16)

            @block.scalar
            def _(act):
                for i, (_, _, hi, _) in enumerate(pieces):
                    act.wait_ge(landed[i % 3], 16 * (i // 3 + 1))
                    act.activation(hi, raw[i % 3][:, :], ACT.Copy).then_inc(hi_ready, 1)

            @block.vector
            def _(dve):
                for i, (_, _, hi, lo) in enumerate(pieces):
                    dve.wait_ge(hi_ready, i + 1)
                    dve.tensor_tensor(lo, raw[i % 3][:, :], hi.bitcast(F32), ALU.subtract).then_inc(lo_ready, 1)


def attention(nc, name, cross, x_rows, ctx_rows, mask, wq, wk, wv, wo, bo, g, beta, out_rows):
    with ExitStack() as ctx:
        def sb(n, shape, dt=F32):
            return ctx.enter_context(nc.sbuf_tensor(f"{name}_{n}", shape, dt))

        def psum(n):
            return ctx.enter_context(nc.psum_tensor(f"{name}_{n}", [P, 512], F32))

        def sem(n):
            return ctx.enter_context(nc.semaphore(f"{name}_{n}"))

        def split(n, shape):
            return sb(n + "_hi", shape, F32R), sb(n + "_lo", shape, F32R)

        WQ, WK, WV, WO = (split(n, [P, KC * INNER]) for n in ("wq", "wk", "wv", "wo"))
        load_weights(nc, list(zip((wq, wk, wv, wo), (WQ, WK, WV, WO))), name)

        def wpart(W, c, a, b):
            return tuple(w[:, c * INNER + a:c * INNER + b] for w in W)

        NSRC = 2 if cross else 1
        xin = [sb(f"xin{i}", [P, ST, D]) for i in range(NSRC)]
        qrow = sb("qrow", [P, ST, D]) if not cross else xin[0]
        resid = sb("resid", [P, ST, D])
        XT = [split(f"xt{i}", [P, KC, S]) for i in range(NSRC)]
        QT, KVT = XT[0], XT[-1]
        VP = split("vpad", [P, 2, ST, HG, P])
        QK = split("qk", [P, 2, 2, S])
        SM = sb("scores", [P, 2, ST, S])
        PR = sb("probs", [P, 2, ST, S])
        PT = split("probs_t", [P, 2, ST, S])
        OT = split("heads_t", [P, PAIRS, S])
        y, ywork, yout = sb("y", [P, ST, D]), sb("ywork", [P, ST, D]), sb("yout", [P, ST, D])
        mask8, maskf = sb("mask8", [P, T], U8), sb("maskf", [P, S])
        bo_b, g_b, beta_b = sb("bo_b", [P, D]), sb("g_b", [P, D]), sb("beta_b", [P, D])
        ident = sb("ident", [P, P])
        mx, nb, sums, inv = (sb(n, [P, 2, ST]) for n in ("mx", "nb", "sums", "inv"))
        stat, statx = sb("stat", [P, 5, ST]), sb("statx", [P, 5, ST])
        mhalf = sb("mhalf", [P, ST])
        ps_pj = [psum(f"ps_pj{i}") for i in range(2)]
        ps_s = [psum(f"ps_s{i}") for i in range(2)]
        ps_t = [psum(f"ps_t{i}") for i in range(2)]
        ps_pv, ps_aux = psum("ps_pv"), psum("ps_aux")

        const_in, id_ready, pad_ready, half_ready = sem("const_in"), sem("id_ready"), sem("pad_ready"), sem("half_ready")
        x_in = [sem(f"x_in{i}") for i in range(NSRC)]
        y_stored, y_ready = sem("y_stored"), sem("y_ready")
        resid_ready, qrow_ready = sem("resid_ready"), sem("qrow_ready")
        tr_done, tr_hi, tr_lo = sem("tr_done"), sem("tr_hi"), sem("tr_lo")
        pj_done, pj_hi, pj_lo = sem("pj_done"), sem("pj_hi"), sem("pj_lo")
        s_done, max_ready, exp_ready, norm_ready = sem("s_done"), sem("max_ready"), sem("exp_ready"), sem("norm_ready")
        t_done, t_hi, t_lo = sem("t_done"), sem("t_hi"), sem("t_lo")
        pv_done, o_hi, o_lo = sem("pv_done"), sem("o_hi"), sem("o_lo")
        out_done, out_used = sem("out_done"), sem("out_used")
        veps_ready, rstd_ready = sem("veps_ready"), sem("rstd_ready")
        vepsx_ready, rstdx_ready = sem("vepsx_ready"), sem("rstdx_ready")
        dve_links, dve_gate, pool_gate = sem("dve_links"), sem("dve_gate"), sem("pool_gate")

        NPJ = GROUPS + PAIRS
        PJ = [("v", 0, -1), ("qk", 0, -1), ("qk", 1, -1)]
        for n in range(H):
            if n % HG == 1 and n // HG + 1 < GROUPS:
                PJ.append(("v", n // HG + 1, n))
            if n % 2 == 1 and (n + 3) // 2 < PAIRS:
                PJ.append(("qk", (n + 3) // 2, n))
        assert len(PJ) == NPJ

        def projections(step):
            return [(m, what, k) for m, (what, k, at) in enumerate(PJ) if at == step]

        block = ctx.enter_context(nc.Block())

        @block.sync
        def _(sp):
            for dst, src in ((bo_b, bo), (g_b, g), (beta_b, beta)):
                sp.dma_start(dst[:, :], src.partition_broadcast(P)).then_inc(const_in, 16)
            sp.dma_start(mask8[:, :], mask.rearrange("b s -> (b s)").partition_broadcast(P)).then_inc(const_in, 16)

        @block.gpsimd
        def _(pool):
            make_identity(pool, ident[:, :], id_ready)
            pool.memset(mhalf[:, :], -0.5).then_inc(half_ready, 1)
            for vp in VP:
                pool.memset(vp[:, :, :, :, :].rearrange("p a b c d -> p (a b c d)").bitcast(F32), 0.0).then_inc(pad_ready, 1)
            pool.wait_ge(half_ready, 1)

            def load(rows, first=False):
                for i, src in enumerate((x_rows, ctx_rows)[:NSRC]):
                    pool.dma_start(xin[i][:, :, :], src(rows)).then_inc(x_in[i], 16)

            def power(st, ready, done, at):
                pool.wait_ge(ready, at)
                pool.tensor_tensor(st[:, 4, :], st[:, 3, :], mhalf[:, :], ALU.pow).then_inc(done, 1)

            load(0)
            if not cross:
                power(statx, vepsx_ready, rstdx_ready, 1)
            pool.wait_ge(const_in, 64)
            with pool.Fori(0, B) as b:
                pool.wait_ge(qrow_ready, b + 1)
                pool.wait_ge(out_used, b + 1)
                pool.sem_inc(pool_gate, 1)
                for t in range(ST):
                    pool.tensor_tensor(resid[:, t, :], qrow[:, t, :], bo_b[:, :], ALU.add).then_inc(resid_ready, 1)
                pool.wait_ge(resid_ready, ST * (b + 1))
                pool.wait_ge(tr_done, NSRC * (b + 1))
                pool.sem_inc(pool_gate, 1)
                nxt = pool.snap((b + 1) % B)
                load(nxt)
                if not cross:
                    power(statx, vepsx_ready, rstdx_ready, b + 2)
                power(stat, veps_ready, rstd_ready, b + 1)
                pool.wait_ge(y_ready, b + 1)
                pool.sem_inc(pool_gate, 1)
                pool.dma_start(out_rows(b), yout[:, :, :]).then_inc(y_stored, 16)
                pool.wait_ge(y_stored, 16 * (b + 1))
                pool.sem_inc(pool_gate, 1)
            for i in range(NSRC):
                pool.wait_ge(x_in[i], 16 * (B + 1))

        @block.tensor
        def _(pe):
            def transposes(at):
                for i in range(NSRC):
                    if cross:
                        pe.wait_ge(x_in[i], 16 * at)
                    else:
                        pe.wait_ge(qrow_ready, at)
                    if i:
                        pe.wait_ge(tr_lo, NSRC * (at - 1) + i)
                    src = (qrow if i == 0 else xin[i])
                    for c in range(KC):
                        for t in range(ST):
                            last = pe.transpose(ps_aux[:, c * S + t * P:c * S + (t + 1) * P],
                                                src[:, t, c * P:(c + 1) * P], ident[:, :])
                    last.then_inc(tr_done, 1)

            pe.wait_ge(id_ready, 2)
            transposes(1)
            with pe.Fori(0, B) as b:
                pe.wait_ge(tr_lo, NSRC * (b + 1))

                def project(m, what, k):
                    bank = ps_pj[m % 2]
                    if m >= 2:
                        pe.wait_ge(pj_lo, NPJ * b + m - 1)
                    if what == "v":
                        for t in range(ST):
                            for c in range(KC):
                                last = product(pe, bank[:, t * 256:(t + 1) * 256],
                                               tuple(w[:, c, t * P:(t + 1) * P] for w in KVT),
                                               wpart(WV, c, k * 256, (k + 1) * 256), c == 0 and t == 0, c == KC - 1)
                    else:
                        for j, (W, X) in enumerate(((WQ, QT), (WK, KVT))):
                            for c in range(KC):
                                last = product(pe, bank[:, j * S:(j + 1) * S], wpart(W, c, k * P, (k + 1) * P),
                                               tuple(x[:, c, :] for x in X), c == 0 and j == 0, c == KC - 1)
                    last.then_inc(pj_done, 1)

                def scores(n):
                    pair, r = n // 2, DH * (n % 2)
                    pe.wait_ge(pj_lo, NPJ * b + 1 + PJ.index(next(x for x in PJ if x[:2] == ("qk", pair))))
                    if n >= 2:
                        pe.wait_ge(max_ready, H * b + n - 1)
                    for t in range(ST):
                        last = product(pe, ps_s[n % 2][:, t * S:(t + 1) * S],
                                       tuple(w[r:r + DH, pair % 2, 0, t * P:(t + 1) * P] for w in QK),
                                       tuple(w[r:r + DH, pair % 2, 1, :] for w in QK), t == 0, t == ST - 1)
                    last.then_inc(s_done, 1)

                def transpose_probs(n):
                    pe.wait_ge(norm_ready, H * b + n + 1)
                    if n >= 2:
                        pe.wait_ge(t_lo, H * b + n - 1)
                    for j in range(ST):
                        for t in range(ST):
                            last = pe.transpose(ps_t[n % 2][:, j * S + t * P:j * S + (t + 1) * P],
                                                PR[:, n % 2, t, j * P:(j + 1) * P], ident[:, :])
                    last.then_inc(t_done, 1)

                def attend(n):
                    pe.wait_ge(t_lo, H * b + n + 1)
                    if n % HG == 0:
                        pe.wait_ge(pj_lo, NPJ * b + 1 + PJ.index(next(x for x in PJ if x[:2] == ("v", n // HG))))
                    if n % 2 == 0 and n >= 2:
                        pe.wait_ge(o_lo, PAIRS * b + n // 2)
                    for j in range(ST):
                        last = product(pe, ps_pv[:, 0:S], tuple(v[:, n // HG % 2, j, n % HG, :] for v in VP),
                                       tuple(p[:, n % 2, j, :] for p in PT),
                                       n % 2 == 0 and j == 0, n % 2 == 1 and j == ST - 1)
                    last.then_inc(pv_done, 1)

                for m, what, k in projections(-1):
                    project(m, what, k)
                scores(0)
                scores(1)
                for n in range(H):
                    for m, what, k in projections(n):
                        project(m, what, k)
                    if n + 2 < H:
                        scores(n + 2)
                    transpose_probs(n)
                    if n:
                        attend(n - 1)
                pe.wait_ge(out_used, b + 1)
                transposes(b + 2)
                attend(H - 1)
                pe.wait_ge(o_lo, PAIRS * (b + 1))
                pe.wait_ge(tr_lo, NSRC * (b + 2))
                for t in range(ST):
                    for c in range(PAIRS):
                        last = product(pe, ps_aux[:, t * D:(t + 1) * D], tuple(o[:, c, t * P:(t + 1) * P] for o in OT),
                                       tuple(w[:, c * D:(c + 1) * D] for w in WO), c == 0 and t == 0, c == PAIRS - 1)
                last.then_inc(out_done, 1)

        def vpad_half(vp, g, t, odd):
            return vp[:, g % 2, t, odd:HG:2, DH * odd:DH * odd + DH]

        def v_half(bank, t, odd):
            return bank[:, t * 256:(t + 1) * 256].rearrange("p (h d) -> p h d", d=DH)[:, odd:HG:2, :]

        @block.scalar
        def _(act):
            def hi_of_transposes(at):
                for i in range(NSRC):
                    act.wait_ge(tr_done, NSRC * (at - 1) + i + 1)
                    act.activation(XT[i][0][:, :, :].rearrange("p c s -> p (c s)"), ps_aux[:, :], ACT.Copy).then_inc(tr_hi, 1)

            hi_of_transposes(1)
            act.wait_ge(pad_ready, 2)
            with act.Fori(0, B) as b:
                def hi_of_projection(m, what, k):
                    act.wait_ge(pj_done, NPJ * b + m + 1)
                    if what == "v":
                        if k >= 2:
                            act.wait_ge(pv_done, H * b + HG * (k - 1))
                        for t in range(ST):
                            for odd in range(2):
                                last = act.activation(vpad_half(VP[0], k, t, odd), v_half(ps_pj[m % 2], t, odd), ACT.Copy)
                    else:
                        if k >= 2:
                            act.wait_ge(s_done, H * b + 2 * (k - 1))
                        last = act.activation(QK[0][:, k % 2, :, :].rearrange("p a s -> p (a s)"), ps_pj[m % 2][:, :], ACT.Copy)
                    last.then_inc(pj_hi, 1)

                def exps(n):
                    act.wait_ge(max_ready, H * b + n + 1)
                    if n >= 2:
                        act.wait_ge(t_done, H * b + n - 1)
                    for t in range(ST):
                        last = act.activation(PR[:, n % 2, t, :], SM[:, n % 2, t, :], ACT.Exp,
                                              bias=nb[:, n % 2, t:t + 1], scale=SCALE, accum_out=sums[:, n % 2, t:t + 1])
                    last.then_inc(exp_ready, 1)

                def hi_of_probs(n):
                    act.wait_ge(t_done, H * b + n + 1)
                    if n >= 2:
                        act.wait_ge(pv_done, H * b + n - 1)
                    act.activation(PT[0][:, n % 2, :, :].rearrange("p a s -> p (a s)"), ps_t[n % 2][:, :], ACT.Copy).then_inc(t_hi, 1)

                def hi_of_pair(pair):
                    act.wait_ge(pv_done, H * b + 2 * pair + 2)
                    if pair == 0:
                        act.wait_ge(out_used, b + 1)
                    act.activation(OT[0][:, pair, :], ps_pv[:, 0:S], ACT.Copy).then_inc(o_hi, 1)

                for m, what, k in projections(-1):
                    hi_of_projection(m, what, k)
                exps(0)
                exps(1)
                for n in range(H):
                    for m, what, k in projections(n):
                        hi_of_projection(m, what, k)
                    if n + 2 < H:
                        exps(n + 2)
                    hi_of_probs(n)
                    if n >= 2 and n % 2 == 0:
                        hi_of_pair(n // 2 - 1)
                hi_of_transposes(b + 2)
                hi_of_pair(PAIRS - 1)

        @block.vector
        def _(dve):
            per_turn = 1 + 4 * H + 1 + norm_links(ST, True) + (0 if cross else norm_links(ST, False))
            start = 0 if cross else norm_links(ST, False)

            def lo_of_transposes(at):
                for i in range(NSRC):
                    dve.wait_ge(tr_hi, NSRC * (at - 1) + i + 1)
                    dve.tensor_tensor(XT[i][1][:, :, :].rearrange("p c s -> p (c s)"), ps_aux[:, :],
                                      XT[i][0][:, :, :].rearrange("p c s -> p (c s)").bitcast(F32),
                                      ALU.subtract).then_inc(tr_lo, 1)

            def prepare(link, at):
                dve.wait_ge(x_in[0], 16 * at)
                if cross:
                    dve.sem_inc(qrow_ready, 1)
                else:
                    layer_norm(dve, link, dve_gate, xin[0][:, :, :], qrow, ywork, xin[0], statx, vepsx_ready,
                               rstdx_ready, at)
                    dve.sem_inc(qrow_ready, 1)

            prepare(Links(dve, dve_links), 1)
            dve.wait_ge(const_in, 64)
            dve.sem_inc(out_used, 1)
            lo_of_transposes(1)
            dve.wait_ge(pad_ready, 2)
            with dve.Fori(0, B) as b:
                link = Links(dve, dve_links, per_turn, b, start)
                link(dve.tensor_scalar(maskf[:, :], mask8[:, bass.ds(b * S, S)], MASKED, None, ALU.mult))

                def lo_of_projection(m, what, k):
                    dve.wait_ge(pj_hi, NPJ * b + m + 1)
                    if what == "v":
                        for t in range(ST):
                            for odd in range(2):
                                last = dve.tensor_tensor(vpad_half(VP[1], k, t, odd), v_half(ps_pj[m % 2], t, odd),
                                                         vpad_half(VP[0], k, t, odd).bitcast(F32), ALU.subtract)
                    else:
                        last = dve.tensor_tensor(QK[1][:, k % 2, :, :].rearrange("p a s -> p (a s)"), ps_pj[m % 2][:, :],
                                                 QK[0][:, k % 2, :, :].rearrange("p a s -> p (a s)").bitcast(F32),
                                                 ALU.subtract)
                    last.then_inc(pj_lo, 1)

                def masked_max(n):
                    dve.wait_ge(s_done, H * b + n + 1)
                    dve.sem_inc(dve_gate, 1)
                    if n >= 2:
                        dve.wait_ge(exp_ready, H * b + n - 1)
                        dve.sem_inc(dve_gate, 1)
                    for t in range(ST):
                        link.mark(dve.tensor_tensor_reduce(SM[:, n % 2, t, :], ps_s[n % 2][:, t * S:(t + 1) * S],
                                                           maskf[:, :], 1.0, LOWEST, ALU.add, ALU.max,
                                                           mx[:, n % 2, t:t + 1]))
                    link.join()
                    dve.tensor_scalar(nb[:, n % 2, :], mx[:, n % 2, :], -SCALE, None, ALU.mult).then_inc(max_ready, 1)

                def normalise(n):
                    dve.wait_ge(exp_ready, H * b + n + 1)
                    dve.sem_inc(dve_gate, 1)
                    link(dve.reciprocal(inv[:, n % 2, :], sums[:, n % 2, :]))
                    for t in range(ST):
                        last = dve.tensor_scalar(PR[:, n % 2, t, :], PR[:, n % 2, t, :], inv[:, n % 2, t:t + 1], None, ALU.mult)
                        if t < ST - 1:
                            link.mark(last)
                    last.then_inc(norm_ready, 1)

                def lo_of_probs(n):
                    dve.wait_ge(t_hi, H * b + n + 1)
                    dve.tensor_tensor(PT[1][:, n % 2, :, :].rearrange("p a s -> p (a s)"), ps_t[n % 2][:, :],
                                      PT[0][:, n % 2, :, :].rearrange("p a s -> p (a s)").bitcast(F32),
                                      ALU.subtract).then_inc(t_lo, 1)

                def lo_of_pair(pair):
                    dve.wait_ge(o_hi, PAIRS * b + pair + 1)
                    dve.tensor_tensor(OT[1][:, pair, :], ps_pv[:, 0:S], OT[0][:, pair, :].bitcast(F32),
                                      ALU.subtract).then_inc(o_lo, 1)

                for m, what, k in projections(-1):
                    lo_of_projection(m, what, k)
                masked_max(0)
                masked_max(1)
                normalise(0)
                for n in range(H):
                    for m, what, k in projections(n):
                        lo_of_projection(m, what, k)
                    if n + 1 < H:
                        normalise(n + 1)
                    if n + 2 < H:
                        masked_max(n + 2)
                    lo_of_probs(n)
                    if n >= 2 and n % 2 == 0:
                        lo_of_pair(n // 2 - 1)
                    if n == H // 2:
                        prepare(link, b + 2)
                lo_of_transposes(b + 2)
                lo_of_pair(PAIRS - 1)
                dve.wait_ge(out_done, b + 1)
                dve.wait_ge(resid_ready, ST * (b + 1))
                ins = dve.tensor_tensor(y[:, :, :].rearrange("p t d -> p (t d)"), ps_aux[:, :],
                                        resid[:, :, :].rearrange("p t d -> p (t d)"), ALU.add)
                link(ins)
                dve.sem_inc(out_used, 1)
                layer_norm(dve, link, dve_gate, y[:, :, :], yout, ywork, y, stat, veps_ready, rstd_ready,
                           b + 1, g_b[:, :], beta_b[:, :])
                dve.sem_inc(y_ready, 1)
                link.close()


def mlp(nc, name, x_rows, h_rows, fc1, fc1_b, fc2, fc2_b, g, beta, w1s, w2s, w3s, wg, logits, normed_rows,
        partial_rows, slot_rows):
    NT, N, BLOCKS = 4, 512, T // 512
    with ExitStack() as ctx:
        def sb(n, shape, dt=F32):
            return ctx.enter_context(nc.sbuf_tensor(f"{name}_{n}", shape, dt))

        def psum(n):
            return ctx.enter_context(nc.psum_tensor(f"{name}_{n}", [P, 512], F32))

        def sem(n):
            return ctx.enter_context(nc.semaphore(f"{name}_{n}"))

        def split(n, shape):
            return sb(n + "_hi", shape, F32R), sb(n + "_lo", shape, F32R)

        FC1, FC2, W1, W2, W3 = (split(n, [P, 2048]) for n in ("fc1", "fc2", "w1", "w2", "w3"))
        load_weights(nc, list(zip((fc1, fc2, w1s, w2s, w3s), (FC1, FC2, W1, W2, W3))), name)
        WG, wg_raw = split("wg", [P, KC * E]), sb("wg_raw", [P, KC, E])
        hin, xin = sb("hin", [P, NT, D]), sb("xin", [P, NT, D])
        XT = split("xt", [P, KC, N])
        GT = split("gt", [P, FC, N])
        G, A = sb("g", [P, 2, N]), sb("a", [P, 2, N])
        y, ywork, ynorm, squares = (sb(n, [P, NT, D]) for n in ("y", "ywork", "ynorm", "squares"))
        x2, xn2, part = (sb(n, [P, NT, D]) for n in ("x2", "xn2", "part"))
        b1, b2_b, g_b, beta_b = sb("b1", [P, FC]), sb("b2_b", [P, D]), sb("g_b", [P, D]), sb("beta_b", [P, D])
        ident, zeros, stat, mhalf = sb("ident", [P, P]), sb("zeros", [P, 768]), sb("stat", [P, 5, NT]), sb("mhalf", [P, NT])
        ps_u, ps_v, ps_d = ([psum(f"ps_{k}{i}") for i in range(2)] for k in "uvd")
        ps_l = psum("ps_l")

        const_in, wg_in, id_ready, half_ready = sem("const_in"), sem("wg_in"), sem("id_ready"), sem("half_ready")
        zero_ready, zeroed = sem("zero_ready"), sem("zeroed")
        h_in, x_in, rows_used = sem("h_in"), sem("x_in"), sem("rows_used")
        xn2_ready, part_ready, xn2_stored, part_stored = sem("xn2_ready"), sem("part_ready"), sem("xn2_stored"), sem("part_stored")
        tr_done, tr_hi, tr_lo = sem("tr_done"), sem("tr_hi"), sem("tr_lo")
        up_done, gelu_ready, act_lo = sem("up_done"), sem("gelu_ready"), sem("act_lo")
        down_done, logits_done, wg_ready = sem("down_done"), sem("logits_done"), sem("wg_ready")
        veps_ready, rstd_ready = sem("veps_ready"), sem("rstd_ready")
        dve_links, dve_gate, pool_gate = sem("dve_links"), sem("dve_gate"), sem("pool_gate")
        block = ctx.enter_context(nc.Block())

        @block.sync
        def _(sp):
            for dst, src in ((b2_b, fc2_b), (g_b, g), (beta_b, beta)):
                sp.dma_start(dst[:, :], src.partition_broadcast(P)).then_inc(const_in, 16)
            with nc.allow_non_contiguous_dma(reason="1024 biases, once"):
                sp.dma_start(b1[:, :], fc1_b.rearrange("(m p) -> p m", p=P)).then_inc(const_in, 16)
            sp.dma_start(wg_raw[:, :, :], wg.rearrange("(c p) e -> p c e", p=P)).then_inc(wg_in, 16)
            sp.wait_ge(zero_ready, 1)
            flat = slot_rows.rearrange("(n p r) d -> n p (r d)", p=P, r=3)
            for i in range(flat.shape[0]):
                sp.dma_start(flat[i], zeros[:, :]).then_inc(zeroed, 16)
            sp.wait_ge(zeroed, 16 * flat.shape[0])

        @block.gpsimd
        def _(pool):
            make_identity(pool, ident[:, :], id_ready)
            pool.memset(zeros[:, :], 0.0).then_inc(zero_ready, 1)
            pool.memset(mhalf[:, :], -0.5).then_inc(half_ready, 1)
            pool.wait_ge(half_ready, 1)

            def load(t):
                pool.dma_start(hin[:, :, :], h_rows(t)).then_inc(h_in, 16)
                pool.dma_start(xin[:, :, :], x_rows(t)).then_inc(x_in, 16)

            load(0)
            with pool.Fori(0, BLOCKS) as t:
                for k in range(2):
                    pool.wait_ge(veps_ready, 2 * t + k + 1)
                    pool.tensor_tensor(stat[:, 4, :], stat[:, 3, :], mhalf[:, :], ALU.pow).then_inc(rstd_ready, 1)
                    if k == 0:
                        pool.wait_ge(rows_used, t + 1)
                        pool.sem_inc(pool_gate, 1)
                        load(pool.snap((t + 1) % BLOCKS))
                pool.wait_ge(xn2_ready, t + 1)
                pool.sem_inc(pool_gate, 1)
                pool.dma_start(normed_rows(t), xn2[:, :, :]).then_inc(xn2_stored, 16)
                pool.wait_ge(part_ready, t + 2)
                pool.sem_inc(pool_gate, 1)
                pool.dma_start(partial_rows(t), part[:, :, :]).then_inc(part_stored, 16)
                pool.wait_ge(xn2_stored, 16 * (t + 1))
                pool.sem_inc(pool_gate, 1)
                pool.wait_ge(part_stored, 16 * (t + 1))
                pool.sem_inc(pool_gate, 1)
            pool.wait_ge(h_in, 16 * (BLOCKS + 1))
            pool.wait_ge(x_in, 16 * (BLOCKS + 1))

        @block.tensor
        def _(pe):
            pe.wait_ge(id_ready, 2)
            pe.wait_ge(wg_ready, 2)
            with pe.Fori(0, BLOCKS) as t:
                for k, (src, ups, down) in enumerate(((hin, ((FC1, ps_u),), FC2), (xn2, ((W1, ps_u), (W2, ps_v)), W3))):
                    if k == 0:
                        pe.wait_ge(h_in, 16 * (t + 1))
                        pe.wait_ge(part_ready, t + 1)
                    else:
                        pe.wait_ge(xn2_ready, t + 1)
                    for c in range(KC):
                        for i in range(NT):
                            last = pe.transpose(ps_d[c][:, i * P:(i + 1) * P], src[:, i, c * P:(c + 1) * P], ident[:, :])
                        last.then_inc(tr_done, 1)
                    pe.wait_ge(tr_lo, 2 * KC * t + KC * (k + 1))
                    if k:
                        for i in range(NT):
                            for c in range(KC):
                                last = product(pe, ps_l[:, i * E:(i + 1) * E], tuple(w[:, c, i * P:(i + 1) * P] for w in XT),
                                               tuple(w[:, c * E:(c + 1) * E] for w in WG), c == 0 and i == 0, c == KC - 1)
                        last.then_inc(logits_done, 1)
                    for m in range(FC):
                        if m >= 2:
                            pe.wait_ge(act_lo, 2 * FC * t + FC * k + m - 1)
                        for W, bank in ups:
                            for c in range(KC):
                                last = product(pe, bank[m % 2][:, :], tuple(w[:, c * FF + m * P:c * FF + (m + 1) * P] for w in W),
                                               tuple(w[:, c, :] for w in XT), c == 0, c == KC - 1)
                        last.then_inc(up_done, 1)
                    for m in range(FC):
                        pe.wait_ge(act_lo, 2 * FC * t + FC * k + m + 1)
                        for i in range(NT):
                            last = product(pe, ps_d[i // 2][:, (i % 2) * D:(i % 2 + 1) * D],
                                           tuple(w[:, m, i * P:(i + 1) * P] for w in GT),
                                           tuple(w[:, m * D:(m + 1) * D] for w in down), m == 0 and i % 2 == 0, m == FC - 1)
                    last.then_inc(down_done, 1)

        @block.scalar
        def _(act):
            act.wait_ge(const_in, 64)
            act.wait_ge(wg_in, 16)
            act.activation(WG[0][:, :], wg_raw[:, :, :].rearrange("p c e -> p (c e)"), ACT.Copy).then_inc(wg_ready, 1)
            with act.Fori(0, BLOCKS) as t:
                for k in range(2):
                    for c in range(KC):
                        act.wait_ge(tr_done, 2 * KC * t + KC * k + c + 1)
                        act.activation(XT[0][:, c, :], ps_d[c][:, :], ACT.Copy).then_inc(tr_hi, 1)
                    for m in range(FC):
                        act.wait_ge(up_done, 2 * FC * t + FC * k + m + 1)
                        if m >= 2:
                            act.wait_ge(act_lo, 2 * FC * t + FC * k + m - 1)
                        act.activation(G[:, m % 2, :], ps_u[m % 2][:, :], ACT.Gelu,
                                       bias=b1[:, m:m + 1] if k == 0 else 0.0).then_inc(gelu_ready, 1)

        @block.vector
        def _(dve):
            per_turn = FC + 2 + NT + norm_links(NT, True) + 1 + norm_links(NT, False) + 2 * FC + 1 + 2
            dve.wait_ge(wg_ready, 1)
            dve.tensor_tensor(WG[1][:, :], wg_raw[:, :, :].rearrange("p c e -> p (c e)"), WG[0][:, :].bitcast(F32),
                              ALU.subtract).then_inc(wg_ready, 1)
            dve.wait_ge(const_in, 64)
            dve.sem_inc(part_ready, 1)
            with dve.Fori(0, BLOCKS) as t:
                link = Links(dve, dve_links, per_turn, t)
                for k in range(2):
                    for c in range(KC):
                        dve.wait_ge(tr_hi, 2 * KC * t + KC * k + c + 1)
                        dve.tensor_tensor(XT[1][:, c, :], ps_d[c][:, :], XT[0][:, c, :].bitcast(F32), ALU.subtract).then_inc(tr_lo, 1)
                    if k:
                        dve.wait_ge(logits_done, t + 1)
                        link(dve.tensor_copy(logits[:, bass.ds(t * NT, NT), :].rearrange("p t e -> p (t e)"), ps_l[:, 0:NT * E]))
                    for m in range(FC):
                        act_in = G[:, m % 2, :]
                        dve.wait_ge(gelu_ready, 2 * FC * t + FC * k + m + 1)
                        if k:
                            dve.wait_ge(up_done, 2 * FC * t + FC * k + m + 1)
                            act_in = A[:, m % 2, :]
                            link(dve.tensor_tensor(act_in, ps_v[m % 2][:, :], G[:, m % 2, :], ALU.mult))
                        link(dve.tensor_copy(GT[0][:, m, :], act_in))
                        dve.tensor_tensor(GT[1][:, m, :], act_in, GT[0][:, m, :].bitcast(F32), ALU.subtract).then_inc(act_lo, 1)
                    dve.wait_ge(down_done, 2 * t + k + 1)
                    rows = (y, part)[k]
                    for i in range(2):
                        if k == 0 and i == 0:
                            dve.wait_ge(x_in, 16 * (t + 1))
                        link.mark(dve.tensor_tensor(rows[:, 2 * i:2 * i + 2, :].rearrange("p t d -> p (t d)"), ps_d[i][:, :],
                                                    (hin, x2)[k][:, 2 * i:2 * i + 2, :].rearrange("p t d -> p (t d)"), ALU.add))
                    link.join()
                    if k == 0:
                        for i in range(NT):
                            link.mark(dve.tensor_tensor(y[:, i, :], y[:, i, :], b2_b[:, :], ALU.add))
                        link.join()
                        layer_norm(dve, link, dve_gate, y[:, :, :], ynorm, ywork, squares, stat, veps_ready, rstd_ready,
                                   2 * t + 1, g_b[:, :], beta_b[:, :])
                        link(dve.tensor_tensor(x2[:, :, :].rearrange("p t d -> p (t d)"), xin[:, :, :].rearrange("p t d -> p (t d)"),
                                               ynorm[:, :, :].rearrange("p t d -> p (t d)"), ALU.add))
                        dve.sem_inc(rows_used, 1)
                        layer_norm(dve, link, dve_gate, x2[:, :, :], xn2, ywork, squares, stat, veps_ready, rstd_ready,
                                   2 * t + 2)
                        dve.sem_inc(xn2_ready, 1)
                    else:
                        dve.sem_inc(part_ready, 1)
                link.close()


def route(nc, logits, position, slot_expert, normed, slot_rows):
    with ExitStack() as ctx:
        def sb(n, shape, dt=F32):
            return ctx.enter_context(nc.sbuf_tensor(f"route_{n}", shape, dt))

        def sem(n):
            return ctx.enter_context(nc.semaphore(f"route_{n}"))

        rows = sb("rows", [P, TT, D])
        expert_no, slot_no, step_no = sb("expert_no", [P, TT, E]), sb("slot_no", [P, SLOTS, E]), sb("step_no", [P, E, T // SLOT])
        before, ones = sb("before", [P, P], BF16), sb("ones", [P, P], BF16)
        top, key, first = sb("top", [P, TT]), sb("key", [P, TT, E]), sb("first", [P, TT])
        chosen, chosen16 = sb("chosen", [P, TT, E]), sb("chosen16", [P, TT, E], BF16)
        of_tile, prefix, where = sb("of_tile", [P, TT, E]), sb("prefix", [P, TT + 1, E]), sb("where", [P, TT, E])
        steps, slots, first_slot = sb("steps", [P, E, T // SLOT]), sb("slots", [P, E]), sb("first_slot", [P, E + 1])
        ended, expert_f, pos_f = sb("ended", [P, SLOTS, E]), sb("expert_f", [P, SLOTS]), sb("pos_f", [P, TT])
        ps = [ctx.enter_context(nc.psum_tensor(f"route_ps{i}", [P, 512], F32)) for i in range(2)]
        rows_in, consts, pool_links, dve_links = sem("rows_in"), sem("consts"), sem("pool_links"), sem("dve_links")
        chosen_ready, counted, pos_ready, scattered = sem("chosen_ready"), sem("counted"), sem("pos_ready"), sem("scattered")
        block = ctx.enter_context(nc.Block())

        @block.sync
        def _(sp):
            sp.dma_start(rows[:, :, :], normed.rearrange("(t p) d -> p t d", p=P)).then_inc(rows_in, 16)

        @block.gpsimd
        def _(pool):
            kw = dict(allow_small_or_imprecise_dtypes=True)
            pool.iota(expert_no[:, :, :], [[0, TT], [1, E]], base=0, channel_multiplier=0, **kw).then_inc(consts, 1)
            pool.iota(slot_no[:, :, :], [[1, SLOTS], [0, E]], base=0, channel_multiplier=0, **kw).then_inc(consts, 1)
            pool.iota(step_no[:, :, :], [[0, E], [SLOT, T // SLOT]], base=0, channel_multiplier=0, **kw).then_inc(consts, 1)
            pool.memset(ones[:, :], 1.0).then_inc(consts, 1)
            pool.memset(before[:, :], 1.0).then_inc(pool_links, 1)
            pool.wait_ge(pool_links, 1)
            pool.affine_select(out=before[:, :], in_=before[:, :], compare_op=ALU.is_gt, fill=0.0, base=0,
                               pattern=[[1, P]], channel_multiplier=-1).then_inc(consts, 1)
            pool.wait_ge(rows_in, 16)
            pool.wait_ge(pos_ready, 1)
            for t in range(TT):
                pool.indirect_dma_start(slot_rows, bass.IndirectOffsetOnAxis(ap=position[:, t:t + 1], axis=0),
                                        rows[:, t, :], None).then_inc(scattered, 16)
            pool.wait_ge(scattered, 16 * TT)

        @block.tensor
        def _(pe):
            pe.wait_ge(consts, 5)
            pe.wait_ge(chosen_ready, 1)
            flat = chosen16[:, :, :].rearrange("p t e -> p (t e)")
            pe.matmul(ps[0][:, 0:TT * E], before[:, :], flat, start=True, stop=True)
            pe.matmul(ps[1][:, 0:TT * E], ones[:, :], flat, start=True, stop=True).then_inc(counted, 1)

        @block.vector
        def _(dve):
            link = Links(dve, dve_links)
            dve.wait_ge(consts, 5)
            over_e = lambda ap: ap.unsqueeze(2).to_broadcast([P, TT, E])
            link(dve.tensor_reduce(top[:, :], logits[:, :, :], AX.X, ALU.max))
            link(dve.tensor_tensor(key[:, :, :], logits[:, :, :], over_e(top[:, :]), ALU.is_equal))
            link(dve.scalar_tensor_tensor(out=key[:, :, :], in0=key[:, :, :], scalar=-float(E), in1=expert_no[:, :, :],
                                          op0=ALU.mult, op1=ALU.add))
            link(dve.tensor_reduce(first[:, :], key[:, :, :], AX.X, ALU.min))
            link(dve.tensor_tensor(chosen[:, :, :], key[:, :, :], over_e(first[:, :]), ALU.is_equal))
            dve.tensor_copy(chosen16[:, :, :], chosen[:, :, :]).then_inc(chosen_ready, 1)
            link(dve.memset(prefix[:, 0, :], 0.0))
            dve.wait_ge(counted, 1)
            link(dve.tensor_copy(of_tile[:, :, :].rearrange("p t e -> p (t e)"), ps[1][:, 0:TT * E]))
            for t in range(TT):
                link(dve.tensor_tensor(prefix[:, t + 1, :], prefix[:, t, :], of_tile[:, t, :], ALU.add))
            link(dve.tensor_tensor(steps[:, :, :], prefix[:, TT, :].unsqueeze(2).to_broadcast([P, E, T // SLOT]),
                                   step_no[:, :, :], ALU.is_gt))
            link(dve.tensor_reduce(slots[:, :], steps[:, :, :], AX.X, ALU.add))
            link(dve.memset(first_slot[:, 0:1], 0.0))
            for e in range(E):
                link(dve.tensor_tensor(first_slot[:, e + 1:e + 2], first_slot[:, e:e + 1], slots[:, e:e + 1], ALU.add))
            link(dve.tensor_tensor(ended[:, :, :], slot_no[:, :, :],
                                   first_slot[:, 1:E + 1].unsqueeze(1).to_broadcast([P, SLOTS, E]), ALU.is_ge))
            link(dve.tensor_reduce(expert_f[:, :], ended[:, :, :], AX.X, ALU.add))
            link(dve.tensor_scalar(slot_expert[:, :], expert_f[:, :], float(E - 1), None, ALU.min))
            link(dve.tensor_tensor(where[:, :, :].rearrange("p t e -> p (t e)"), ps[0][:, 0:TT * E],
                                   prefix[:, 0:TT, :].rearrange("p t e -> p (t e)"), ALU.add))
            link(dve.scalar_tensor_tensor(out=where[:, :, :], in0=first_slot[:, 0:E].unsqueeze(1).to_broadcast([P, TT, E]),
                                          scalar=float(SLOT), in1=where[:, :, :], op0=ALU.mult, op1=ALU.add))
            link(dve.tensor_tensor(where[:, :, :], where[:, :, :], chosen[:, :, :], ALU.mult))
            link(dve.tensor_reduce(pos_f[:, :], where[:, :, :], AX.X, ALU.add))
            dve.tensor_copy(position[:, :], pos_f[:, :]).then_inc(pos_ready, 1)


def experts(nc, slot_expert, w1, w2, w3, slot_rows, slot_out):
    with ExitStack() as ctx:
        def sb(n, shape, dt=F32):
            return ctx.enter_context(nc.sbuf_tensor(f"moe_{n}", shape, dt))

        def psum(n):
            return ctx.enter_context(nc.psum_tensor(f"moe_{n}", [P, 512], F32))

        def sem(n):
            return ctx.enter_context(nc.semaphore(f"moe_{n}"))

        NT = SLOT // P
        raw = sb("raw", [P, 3, 2048])
        WH, WL = sb("w_hi", [P, 3, 2048], F32R), sb("w_lo", [P, 3, 2048], F32R)
        xin, yout, ident = sb("xin", [P, NT, D]), sb("yout", [P, NT, D]), sb("ident", [P, P])
        XT = sb("xt_hi", [P, KC, SLOT], F32R), sb("xt_lo", [P, KC, SLOT], F32R)
        GT = sb("gt_hi", [P, FC, SLOT], F32R), sb("gt_lo", [P, FC, SLOT], F32R)
        G, A = sb("g", [P, 2, SLOT]), sb("a", [P, 2, SLOT])
        ps_u, ps_v, ps_d, ps_t = [psum(f"u{i}") for i in range(2)], [psum(f"v{i}") for i in range(2)], psum("d"), psum("t")
        raw_in = [sem(f"raw_in{i}") for i in range(3)]
        w_hi, w_lo = [sem(f"w_hi{i}") for i in range(3)], [sem(f"w_lo{i}") for i in range(3)]
        id_ready, x_in, tr_done, tr_hi, tr_lo = sem("id_ready"), sem("x_in"), sem("tr_done"), sem("tr_hi"), sem("tr_lo")
        up_done, gelu_ready, act_lo, down_done = sem("up_done"), sem("gelu_ready"), sem("act_lo"), sem("down_done")
        y_ready, y_stored, dve_links = sem("y_ready"), sem("y_stored"), sem("dve_links")
        sp_gate, pool_gate, yout_free = sem("sp_gate"), sem("pool_gate"), sem("yout_free")
        block = ctx.enter_context(nc.Block())
        srcs = (w1.rearrange("e (c p) n -> p e c n", p=P), w2.rearrange("e (c p) n -> p e c n", p=P),
                w3.rearrange("e (c p) n -> p e c n", p=P))

        @block.sync
        def _(sp):
            def load(slot):
                e = sp.value_load(slot_expert[0:1, bass.ds(slot, 1)], min_val=0, max_val=E - 1)
                for k in range(3):
                    n = srcs[k].shape[3]
                    sp.dma_start(raw[:, k, :].rearrange("p (o c n) -> p o c n", o=1, n=n), srcs[k][:, bass.ds(e, 1), :, :])\
                        .then_inc(raw_in[k], 16)

            load(0)
            with sp.Fori(1, SLOTS) as s:
                for k in range(3):
                    sp.wait_ge(w_lo[k], s)
                    sp.sem_inc(sp_gate, 1)
                load(s)

        @block.gpsimd
        def _(pool):
            make_identity(pool, ident[:, :], id_ready)

            def load(s):
                pool.dma_start(xin[:, :, :], slot_rows[bass.ds(s * SLOT, SLOT), :].rearrange("(t p) d -> p t d", p=P))\
                    .then_inc(x_in, 16)

            def lo_of_weights(k, at):
                pool.wait_ge(w_hi[k], at)
                pool.tensor_tensor(WL[:, k, :], raw[:, k, :], WH[:, k, :].bitcast(F32), ALU.subtract).then_inc(w_lo[k], 1)

            def store(s):
                pool.wait_ge(y_ready, s + 2)
                pool.sem_inc(pool_gate, 1)
                pool.dma_start(slot_out[bass.ds(s * SLOT, SLOT), :].rearrange("(t p) d -> p t d", p=P), yout[:, :, :])\
                    .then_inc(y_stored, 16)

            def wait_stored(s):
                pool.wait_ge(y_stored, 16 * (s + 1))
                pool.sem_inc(yout_free, 1)

            pool.sem_inc(yout_free, 1)
            load(0)
            lo_of_weights(1, 1)
            lo_of_weights(2, 1)
            with pool.Fori(0, SLOTS - 1) as s:
                pool.wait_ge(tr_done, s + 1)
                pool.sem_inc(pool_gate, 1)
                load(s + 1)
                lo_of_weights(1, s + 2)
                store(s)
                lo_of_weights(2, s + 2)
                wait_stored(s)
            pool.wait_ge(tr_done, SLOTS)
            load(0)
            store(SLOTS - 1)
            wait_stored(SLOTS - 1)
            pool.wait_ge(x_in, 16 * (SLOTS + 1))

        @block.tensor
        def _(pe):
            def transposes(at):
                pe.wait_ge(x_in, 16 * at)
                for c in range(KC):
                    for t in range(NT):
                        last = pe.transpose(ps_t[:, c * SLOT + t * P:c * SLOT + (t + 1) * P], xin[:, t, c * P:(c + 1) * P], ident[:, :])
                last.then_inc(tr_done, 1)

            pe.wait_ge(id_ready, 2)
            transposes(1)
            with pe.Fori(0, SLOTS) as s:
                pe.wait_ge(tr_lo, s + 1)
                pe.wait_ge(w_lo[0], s + 1)
                pe.wait_ge(w_lo[1], s + 1)
                for m in range(FC):
                    if m >= 2:
                        pe.wait_ge(act_lo, FC * s + m - 1)
                    for k, bank in ((0, ps_u), (1, ps_v)):
                        for c in range(KC):
                            last = product(pe, bank[m % 2][:, 0:SLOT],
                                           tuple(w[:, k, c * FF + m * P:c * FF + (m + 1) * P] for w in (WH, WL)),
                                           tuple(x[:, c, :] for x in XT), c == 0, c == KC - 1)
                    last.then_inc(up_done, 1)
                transposes(s + 2)
                pe.wait_ge(w_lo[2], s + 1)
                pe.wait_ge(y_ready, s + 1)
                for m in range(FC):
                    pe.wait_ge(act_lo, FC * s + m + 1)
                    for t in range(NT):
                        last = product(pe, ps_d[:, t * D:(t + 1) * D], tuple(w[:, m, t * P:(t + 1) * P] for w in GT),
                                       tuple(w[:, 2, m * D:(m + 1) * D] for w in (WH, WL)), m == 0 and t == 0, m == FC - 1)
                last.then_inc(down_done, 1)

        @block.scalar
        def _(act):
            def hi_of_weights(k, at):
                act.wait_ge(raw_in[k], 16 * at)
                act.activation(WH[:, k, :], raw[:, k, :], ACT.Copy).then_inc(w_hi[k], 1)

            def hi_of_transposes(at):
                act.wait_ge(tr_done, at)
                act.activation(XT[0][:, :, :].rearrange("p c s -> p (c s)"), ps_t[:, :], ACT.Copy).then_inc(tr_hi, 1)

            def gelus(s):
                for m in range(FC):
                    act.wait_ge(up_done, FC * s + m + 1)
                    if m >= 2:
                        act.wait_ge(act_lo, FC * s + m - 1)
                    act.activation(G[:, m % 2, :], ps_u[m % 2][:, 0:SLOT], ACT.Gelu).then_inc(gelu_ready, 1)

            hi_of_weights(0, 1)
            hi_of_weights(1, 1)
            hi_of_weights(2, 1)
            hi_of_transposes(1)
            with act.Fori(0, SLOTS - 1) as s:
                gelus(s)
                hi_of_transposes(s + 2)
                hi_of_weights(0, s + 2)
                hi_of_weights(1, s + 2)
                act.wait_ge(down_done, s + 1)
                hi_of_weights(2, s + 2)
            gelus(SLOTS - 1)
            hi_of_transposes(SLOTS + 1)

        @block.vector
        def _(dve):
            per_turn = 2 * FC

            def lo_of_weights(at):
                dve.wait_ge(w_hi[0], at)
                dve.tensor_tensor(WL[:, 0, :], raw[:, 0, :], WH[:, 0, :].bitcast(F32), ALU.subtract).then_inc(w_lo[0], 1)

            def lo_of_transposes(at):
                dve.wait_ge(tr_hi, at)
                dve.tensor_tensor(XT[1][:, :, :].rearrange("p c s -> p (c s)"), ps_t[:, :],
                                  XT[0][:, :, :].rearrange("p c s -> p (c s)").bitcast(F32), ALU.subtract).then_inc(tr_lo, 1)

            def hidden(s):
                link = Links(dve, dve_links, per_turn, s)
                for m in range(FC):
                    dve.wait_ge(gelu_ready, FC * s + m + 1)
                    dve.wait_ge(up_done, FC * s + m + 1)
                    link(dve.tensor_tensor(A[:, m % 2, :], ps_v[m % 2][:, 0:SLOT], G[:, m % 2, :], ALU.mult))
                    link(dve.tensor_copy(GT[0][:, m, :], A[:, m % 2, :]))
                    dve.tensor_tensor(GT[1][:, m, :], A[:, m % 2, :], GT[0][:, m, :].bitcast(F32), ALU.subtract).then_inc(act_lo, 1)
                link.close()

            def store(s):
                dve.wait_ge(down_done, s + 1)
                dve.wait_ge(yout_free, s + 1)
                dve.tensor_copy(yout[:, :, :].rearrange("p t d -> p (t d)"), ps_d[:, :]).then_inc(y_ready, 1)

            dve.sem_inc(y_ready, 1)
            lo_of_weights(1)
            lo_of_transposes(1)
            with dve.Fori(0, SLOTS - 1) as s:
                hidden(s)
                lo_of_transposes(s + 2)
                lo_of_weights(s + 2)
                store(s)
            hidden(SLOTS - 1)
            lo_of_transposes(SLOTS + 1)
            store(SLOTS - 1)


def combine(nc, position, partial, slot_out, out):
    with ExitStack() as ctx:
        part = ctx.enter_context(nc.sbuf_tensor("comb_part", [P, TT, D], F32))
        rows = ctx.enter_context(nc.sbuf_tensor("comb_rows", [P, TT, D], F32))
        part_in, summed, stored = (ctx.enter_context(nc.semaphore(f"comb_{n}")) for n in ("part_in", "summed", "stored"))
        gathered = [ctx.enter_context(nc.semaphore(f"comb_gathered{q}")) for q in range(TT // 4)]
        out_v = out.rearrange("(t p) d -> p t d", p=P)
        block = ctx.enter_context(nc.Block())

        @block.sync
        def _(sp):
            sp.dma_start(part[:, :, :], partial.rearrange("(t p) d -> p t d", p=P)).then_inc(part_in, 16)
            for q in range(0, TT, 4):
                sp.wait_ge(summed, q + 4)
                sp.dma_start(out_v[:, q:q + 4, :], part[:, q:q + 4, :]).then_inc(stored, 16)
            sp.wait_ge(stored, 16 * (TT // 4))

        @block.gpsimd
        def _(pool):
            for t in range(TT):
                pool.indirect_dma_start(rows[:, t, :], None, slot_out,
                                        bass.IndirectOffsetOnAxis(ap=position[:, t:t + 1], axis=0)).then_inc(gathered[t // 4], 16)

        @block.vector
        def _(dve):
            dve.wait_ge(part_in, 16)
            for t in range(TT):
                if t % 4 == 0:
                    dve.wait_ge(gathered[t // 4], 64)
                dve.tensor_tensor(part[:, t, :], part[:, t, :], rows[:, t, :], ALU.add).then_inc(summed, 1)


def rows_of_batch(x):
    return lambda b: x[bass.ds(b * S, S), :].rearrange("(t p) d -> p t d", p=P)


def rows_of_block(x):
    return lambda t: x[bass.ds(t * 512, 512), :].rearrange("(t p) d -> p t d", p=P)


def build(nc, a, out):
    flat = lambda ap: ap.rearrange("b s d -> (b s) d")
    xa = lambda n: a["L0_xattn_" + n]
    ff = lambda n: a["L0_ffn_" + n]
    scratch = lambda n, rows: nc.dram_tensor(n, (rows, D), F32, kind="Internal").ap()
    after_self, after_cross, normed, partial = (scratch(n, T) for n in ("after_self", "after_cross", "normed", "partial"))
    slot_rows, slot_out = scratch("slot_rows", SLOTS * SLOT), scratch("slot_out", SLOTS * SLOT)
    x, context, mask = flat(a["x"]), flat(a["ctx_1024"]), a["mask_BxS2_bk0"]
    attention(nc, "sa", False, rows_of_batch(x), None, mask, xa("sa_wq"), xa("sa_wk"), xa("sa_wv"), xa("sa_wo"),
              xa("sa_bo"), xa("ln1_g"), xa("ln1_b"), rows_of_batch(after_self))
    attention(nc, "ca", True, rows_of_batch(after_self), rows_of_batch(context), mask, xa("ca_wq"), xa("ca_wk"),
              xa("ca_wv"), xa("ca_wo"), xa("ca_bo"), xa("ln2_g"), xa("ln2_b"), rows_of_batch(after_cross))
    with (nc.sbuf_tensor("logits", [P, TT, E], F32) as logits, nc.sbuf_tensor("position", [P, TT], I32) as position,
          nc.sbuf_tensor("slot_expert", [P, SLOTS], I32) as slot_expert):
        mlp(nc, "mlp", rows_of_block(x), rows_of_block(after_cross), xa("fc1_w"), xa("fc1_b"), xa("fc2_w"), xa("fc2_b"),
            xa("ln3_g"), xa("ln3_b"), ff("w1s"), ff("w2s"), ff("w3s"), ff("Wg"), logits, rows_of_block(normed),
            rows_of_block(partial), slot_rows)
        route(nc, logits, position, slot_expert, normed, slot_rows)
        experts(nc, slot_expert, ff("W1"), ff("W2"), ff("W3"), slot_rows, slot_out)
        combine(nc, position, partial, slot_out, flat(out))


_OUTS = [((B, S, D), "float32")]


def kernel(**inputs):
    import numpy as _np
    import concourse.bacc as _bacc
    from concourse.bass_utils import run_bass_kernel_spmd as _run

    nc = _bacc.Bacc("TRN2", target_bir_lowering=False, num_devices=1)
    arrays, args = {}, {}
    for name, a in inputs.items():
        a = _np.ascontiguousarray(a)
        arrays[f"in_{name}"] = a
        args[name] = nc.dram_tensor(f"in_{name}", a.shape, mybir.dt.from_np(a.dtype), kind="ExternalInput").ap()
    outs = [nc.dram_tensor(f"out_{i}", shape, mybir.dt.from_np(_np.dtype(dt)), kind="ExternalOutput").ap()
            for i, (shape, dt) in enumerate(_OUTS)]
    build(nc, args, outs[0])
    r = _run(nc, [arrays], core_ids=[0])
    return r.results[0]["out_0"]
```

```python
from contextlib import ExitStack

import concourse.bass as bass
from concourse import mybir

F32 = mybir.dt.float32
F32R = mybir.dt.float32r
BF16 = mybir.dt.bfloat16
I32 = mybir.dt.int32
U8 = mybir.dt.uint8
ACT = mybir.ActivationFunctionType
ALU = mybir.AluOpType
AX = mybir.AxisListType

P = 128
B, S, D = 8, 256, 256
T = B * S
H, DH = 16, 64
INNER = H * DH
FF = 1024
E = 8
KC = D // P
ST = S // P
PAIRS = H // 2
GROUPS = 4
HG = H // GROUPS
FC = FF // P
EPS = 1e-5
SCALE = DH ** -0.5
MASKED = -(2.0 ** 126)
LOWEST = -3.0e38
SLOT = 256
SLOTS = T // SLOT + E - 1
TT = T // P


class Links:

    def __init__(self, eng, sem, per_turn=0, turn=0, before=0):
        self.eng, self.sem, self.per_turn, self.turn, self.before, self.n = eng, sem, per_turn, turn, before, 0

    def mark(self, ins):
        ins.then_inc(self.sem, 1)
        self.n += 1

    def join(self):
        self.eng.wait_ge(self.sem, self.turn * self.per_turn + (self.before + self.n))

    def __call__(self, ins):
        self.mark(ins)
        self.join()

    def close(self):
        assert self.n == self.per_turn, (self.n, self.per_turn)


def product(pe, out, stationary, moving, start, stop):
    (wh, wl), (mh, ml) = stationary, moving
    pe.matmul(out, wl, mh, start=start, stop=False, skip_group_check=True)
    pe.matmul(out, wh, ml, start=False, stop=False, skip_group_check=True)
    return pe.matmul(out, wh, mh, start=False, stop=stop, skip_group_check=True)


def make_identity(pool, ident, sem):
    pool.memset(ident, 0.0).then_inc(sem, 1)
    pool.wait_ge(sem, 1)
    pool.affine_select(out=ident, in_=ident, compare_op=ALU.not_equal, fill=1.0, base=0,
                       pattern=[[-1, P]], channel_multiplier=1).then_inc(sem, 1)


def layer_norm(dve, link, gate, x, out, work, squares, stat, veps_ready, rstd_ready, rstd_at, g=None, beta=None):
    n = x.shape[1]
    total, nmean, ssq, veps, rstd = (stat[:, k, 0:n] for k in range(5))
    link(dve.tensor_reduce(total, x, AX.X, ALU.add))
    link(dve.tensor_scalar(nmean, total, -1.0 / D, None, ALU.mult))
    for t in range(n):
        link.mark(dve.tensor_scalar(work[:, t, :], x[:, t, :], nmean[:, t:t + 1], None, ALU.add))
    for t in range(n):
        link.join()
        dve.sem_inc(gate, 1)
        link.mark(dve.tensor_tensor_reduce(squares[:, t, :], work[:, t, :], work[:, t, :], 1.0, 0.0,
                                           ALU.mult, ALU.add, ssq[:, t:t + 1]))
    link.join()
    dve.tensor_scalar(veps, ssq, 1.0 / D, EPS, ALU.mult, ALU.add).then_inc(veps_ready, 1)
    dve.wait_ge(rstd_ready, rstd_at)
    for t in range(n):
        if g is None:
            link.mark(dve.tensor_scalar(out[:, t, :], work[:, t, :], rstd[:, t:t + 1], None, ALU.mult))
        else:
            link.mark(dve.scalar_tensor_tensor(out=out[:, t, :], in0=work[:, t, :],
                                               scalar=rstd[:, t:t + 1], in1=g, op0=ALU.mult, op1=ALU.mult))
    if g is not None:
        link.join()
        for t in range(n):
            link.mark(dve.tensor_tensor(out[:, t, :], out[:, t, :], beta, ALU.add))
    link.join()


def norm_links(n, affine):
    return 2 + 3 * n + (n if affine else 0)


def load_weights(nc, weights, prefix):
    PIECE = 2048
    with ExitStack() as ctx:
        raw = [ctx.enter_context(nc.sbuf_tensor(f"{prefix}_raw{i}", [P, PIECE], F32)) for i in range(3)]
        landed = [ctx.enter_context(nc.semaphore(f"{prefix}_landed{i}")) for i in range(3)]
        hi_ready = ctx.enter_context(nc.semaphore(f"{prefix}_hi_ready"))
        lo_ready = ctx.enter_context(nc.semaphore(f"{prefix}_lo_ready"))
        pieces = []
        for w, (hi, lo) in weights:
            k, n = w.shape
            step = PIECE // n
            for c in range(0, k // P, step):
                pieces.append((w.rearrange("(c p) n -> p c n", p=P)[:, c:c + step, :], n,
                               hi[:, c * n:(c + step) * n], lo[:, c * n:(c + step) * n]))
        with nc.Block() as block:
            @block.sync
            def _(sp):
                for i, (src, n, _, _) in enumerate(pieces):
                    if i >= 3:
                        sp.wait_ge(lo_ready, i - 2)
                    sp.dma_start(raw[i % 3][:, :].rearrange("p (c n) -> p c n", n=n), src).then_inc(landed[i % 3], 16)

            @block.scalar
            def _(act):
                for i, (_, _, hi, _) in enumerate(pieces):
                    act.wait_ge(landed[i % 3], 16 * (i // 3 + 1))
                    act.activation(hi, raw[i % 3][:, :], ACT.Copy).then_inc(hi_ready, 1)

            @block.vector
            def _(dve):
                for i, (_, _, hi, lo) in enumerate(pieces):
                    dve.wait_ge(hi_ready, i + 1)
                    dve.tensor_tensor(lo, raw[i % 3][:, :], hi.bitcast(F32), ALU.subtract).then_inc(lo_ready, 1)


def attention(nc, name, cross, x_rows, ctx_rows, mask, wq, wk, wv, wo, bo, g, beta, out_rows):
    with ExitStack() as ctx:
        def sb(n, shape, dt=F32):
            return ctx.enter_context(nc.sbuf_tensor(f"{name}_{n}", shape, dt))

        def psum(n):
            return ctx.enter_context(nc.psum_tensor(f"{name}_{n}", [P, 512], F32))

        def sem(n):
            return ctx.enter_context(nc.semaphore(f"{name}_{n}"))

        def split(n, shape):
            return sb(n + "_hi", shape, F32R), sb(n + "_lo", shape, F32R)

        WQ, WK, WV, WO = (split(n, [P, KC * INNER]) for n in ("wq", "wk", "wv", "wo"))
        load_weights(nc, list(zip((wq, wk, wv, wo), (WQ, WK, WV, WO))), name)

        def wpart(W, c, a, b):
            return tuple(w[:, c * INNER + a:c * INNER + b] for w in W)

        NSRC = 2 if cross else 1
        xin = [sb(f"xin{i}", [P, ST, D]) for i in range(NSRC)]
        qrow = sb("qrow", [P, ST, D]) if not cross else xin[0]
        resid = sb("resid", [P, ST, D])
        XT = [split(f"xt{i}", [P, KC, S]) for i in range(NSRC)]
        QT, KVT = XT[0], XT[-1]
        VP = split("vpad", [P, 2, ST, HG, P])
        QK = split("qk", [P, 2, 2, S])
        SM = sb("scores", [P, 2, ST, S])
        PR = sb("probs", [P, 2, ST, S])
        PT = split("probs_t", [P, 2, ST, S])
        OT = split("heads_t", [P, PAIRS, S])
        y, ywork, yout = sb("y", [P, ST, D]), sb("ywork", [P, ST, D]), sb("yout", [P, ST, D])
        mask8, maskf = sb("mask8", [P, T], U8), sb("maskf", [P, S])
        bo_b, g_b, beta_b = sb("bo_b", [P, D]), sb("g_b", [P, D]), sb("beta_b", [P, D])
        ident = sb("ident", [P, P])
        mx, nb, sums, inv = (sb(n, [P, 2, ST]) for n in ("mx", "nb", "sums", "inv"))
        stat, statx = sb("stat", [P, 5, ST]), sb("statx", [P, 5, ST])
        mhalf = sb("mhalf", [P, ST])
        ps_pj = [psum(f"ps_pj{i}") for i in range(2)]
        ps_s = [psum(f"ps_s{i}") for i in range(2)]
        ps_t = [psum(f"ps_t{i}") for i in range(2)]
        ps_pv, ps_aux = psum("ps_pv"), psum("ps_aux")

        const_in, id_ready, pad_ready, half_ready = sem("const_in"), sem("id_ready"), sem("pad_ready"), sem("half_ready")
        x_in = [sem(f"x_in{i}") for i in range(NSRC)]
        y_stored, y_ready = sem("y_stored"), sem("y_ready")
        resid_ready, qrow_ready = sem("resid_ready"), sem("qrow_ready")
        tr_done, tr_hi, tr_lo = sem("tr_done"), sem("tr_hi"), sem("tr_lo")
        pj_done, pj_hi, pj_lo = sem("pj_done"), sem("pj_hi"), sem("pj_lo")
        s_done, max_ready, exp_ready, norm_ready = sem("s_done"), sem("max_ready"), sem("exp_ready"), sem("norm_ready")
        inv_ready, norm2_ready = sem("inv_ready"), sem("norm2_ready")
        t_done, t_hi, t_lo = sem("t_done"), sem("t_hi"), sem("t_lo")
        pv_done, o_hi, o_lo = sem("pv_done"), sem("o_hi"), sem("o_lo")
        out_done, out_used = sem("out_done"), sem("out_used")
        veps_ready, rstd_ready = sem("veps_ready"), sem("rstd_ready")
        vepsx_ready, rstdx_ready = sem("vepsx_ready"), sem("rstdx_ready")
        dve_links, dve_gate, pool_gate = sem("dve_links"), sem("dve_gate"), sem("pool_gate")

        NPJ = GROUPS + PAIRS
        PJ = [("v", 0, H - 3), ("qk", 0, H - 3), ("qk", 1, H - 1)]
        for n in range(H - 3):
            if n % HG == 1:
                PJ.append(("v", n // HG + 1, n))
            if n % 2 == 1:
                PJ.append(("qk", (n + 3) // 2, n))
        AHEAD = 3
        assert len(PJ) == NPJ
        OUT_AT, SUM_AT, RESID_AT, LOAD_AT, NORM_AT, STORE_AT, PREPARE_AT, TRANSPOSE_AT = 1, 2, 3, 4, 4, 5, 7, H - 5

        def projections(step, last):
            return [(int(m < AHEAD), m, what, k) for m, (what, k, at) in enumerate(PJ)
                    if at == step and not (last and m < AHEAD)]

        def projected(what, k):
            return 1 + next(m for m, x in enumerate(PJ) if x[:2] == (what, k))

        def ahead(b, n, last):
            if n < H:
                return [(b, n)]
            return [] if last else [(b + 1, n - H)]

        def wait(eng, sem, value):
            if not (isinstance(value, int) and value <= 0):
                eng.wait_ge(sem, value)

        def turns(eng, turn):
            turn(0, True, False)
            with eng.Fori(1, B - 1) as b:
                turn(b, False, False)
            turn(B - 1, False, True)

        block = ctx.enter_context(nc.Block())

        @block.sync
        def _(sp):
            for dst, src in ((bo_b, bo), (g_b, g), (beta_b, beta)):
                sp.dma_start(dst[:, :], src.partition_broadcast(P)).then_inc(const_in, 16)
            sp.dma_start(mask8[:, :], mask.rearrange("b s -> (b s)").partition_broadcast(P)).then_inc(const_in, 16)

        @block.gpsimd
        def _(pool):
            make_identity(pool, ident[:, :], id_ready)
            pool.memset(mhalf[:, :], -0.5).then_inc(half_ready, 1)
            for vp in VP:
                pool.memset(vp[:, :, :, :, :].rearrange("p a b c d -> p (a b c d)").bitcast(F32), 0.0).then_inc(pad_ready, 1)
            pool.wait_ge(half_ready, 1)

            def load(b):
                for i, src in enumerate((x_rows, ctx_rows)[:NSRC]):
                    pool.dma_start(xin[i][:, :, :], src(b)).then_inc(x_in[i], 16)

            def power(st, ready, done, at):
                pool.wait_ge(ready, at)
                pool.tensor_tensor(st[:, 4, :], st[:, 3, :], mhalf[:, :], ALU.pow).then_inc(done, 1)

            def normalise(b, n):
                pool.wait_ge(inv_ready, H * b + n + 1)
                pool.sem_inc(pool_gate, 1)
                pool.tensor_scalar(PR[:, n % 2, 0, :], PR[:, n % 2, 0, :], inv[:, n % 2, 0:1], None, ALU.mult)\
                    .then_inc(norm_ready, 1)

            def store(b):
                pool.wait_ge(y_ready, b + 1)
                pool.sem_inc(pool_gate, 1)
                pool.dma_start(out_rows(b), yout[:, :, :]).then_inc(y_stored, 16)

            def turn(b, first, last):
                for n in range(H):
                    for at in ahead(b, n + 1, last):
                        normalise(*at)
                    if n == RESID_AT:
                        pool.wait_ge(qrow_ready, b + 1)
                        pool.wait_ge(out_used, b + 1)
                        for t in range(ST):
                            pool.tensor_tensor(resid[:, t, :], qrow[:, t, :], bo_b[:, :], ALU.add).then_inc(resid_ready, 1)
                    if n == LOAD_AT and not last:
                        pool.wait_ge(resid_ready, ST * (b + 1))
                        pool.wait_ge(tr_done, NSRC * (b + 1))
                        pool.sem_inc(pool_gate, 1)
                        load(b + 1)
                    if n == NORM_AT and not first:
                        power(stat, veps_ready, rstd_ready, b)
                    if n == STORE_AT and not first:
                        store(b - 1)
                    if n == PREPARE_AT and not cross and not last:
                        power(statx, vepsx_ready, rstdx_ready, b + 2)
                    if n == H - 2 and not first:
                        pool.wait_ge(y_stored, 16 * b)
                        pool.sem_inc(pool_gate, 1)

            load(0)
            if not cross:
                power(statx, vepsx_ready, rstdx_ready, 1)
            pool.wait_ge(const_in, 64)
            normalise(0, 0)
            turns(pool, turn)
            power(stat, veps_ready, rstd_ready, B)
            store(B - 1)
            pool.wait_ge(y_stored, 16 * B)

        @block.tensor
        def _(pe):
            def transposes(b):
                for i in range(NSRC):
                    if cross:
                        pe.wait_ge(x_in[i], 16 * (b + 1))
                    else:
                        pe.wait_ge(qrow_ready, b + 1)
                    if i:
                        pe.wait_ge(tr_lo, NSRC * b + i)
                    src = (qrow if i == 0 else xin[i])
                    for c in range(KC):
                        for t in range(ST):
                            last = pe.transpose(ps_aux[:, c * S + t * P:c * S + (t + 1) * P],
                                                src[:, t, c * P:(c + 1) * P], ident[:, :])
                    last.then_inc(tr_done, 1)

            def project(b, m, what, k):
                bank = ps_pj[m % 2]
                pe.wait_ge(tr_lo, NSRC * (b + 1))
                wait(pe, pj_lo, NPJ * b + m - 1)
                if what == "v":
                    for t in range(ST):
                        for c in range(KC):
                            last = product(pe, bank[:, t * 256:(t + 1) * 256],
                                           tuple(w[:, c, t * P:(t + 1) * P] for w in KVT),
                                           wpart(WV, c, k * 256, (k + 1) * 256), c == 0 and t == 0, c == KC - 1)
                else:
                    for j, (W, X) in enumerate(((WQ, QT), (WK, KVT))):
                        for c in range(KC):
                            last = product(pe, bank[:, j * S:(j + 1) * S], wpart(W, c, k * P, (k + 1) * P),
                                           tuple(x[:, c, :] for x in X), c == 0 and j == 0, c == KC - 1)
                last.then_inc(pj_done, 1)

            def scores(b, n):
                pair, r = n // 2, DH * (n % 2)
                pe.wait_ge(pj_lo, NPJ * b + projected("qk", pair))
                wait(pe, max_ready, H * b + n - 1)
                for t in range(ST):
                    last = product(pe, ps_s[n % 2][:, t * S:(t + 1) * S],
                                   tuple(w[r:r + DH, pair % 2, 0, t * P:(t + 1) * P] for w in QK),
                                   tuple(w[r:r + DH, pair % 2, 1, :] for w in QK), t == 0, t == ST - 1)
                last.then_inc(s_done, 1)

            def transpose_probs(b, n):
                pe.wait_ge(norm_ready, H * b + n + 1)
                pe.wait_ge(norm2_ready, H * b + n + 1)
                wait(pe, t_lo, H * b + n - 1)
                for j in range(ST):
                    for t in range(ST):
                        last = pe.transpose(ps_t[n % 2][:, j * S + t * P:j * S + (t + 1) * P],
                                            PR[:, n % 2, t, j * P:(j + 1) * P], ident[:, :])
                last.then_inc(t_done, 1)

            def attend(b, n):
                pe.wait_ge(t_lo, H * b + n + 1)
                if n % HG == 0:
                    pe.wait_ge(pj_lo, NPJ * b + projected("v", n // HG))
                if n % 2 == 0:
                    wait(pe, o_lo, PAIRS * b + n // 2)
                for j in range(ST):
                    last = product(pe, ps_pv[:, 0:S], tuple(v[:, n // HG % 2, j, n % HG, :] for v in VP),
                                   tuple(p[:, n % 2, j, :] for p in PT),
                                   n % 2 == 0 and j == 0, n % 2 == 1 and j == ST - 1)
                last.then_inc(pv_done, 1)

            def output(b):
                pe.wait_ge(o_lo, PAIRS * (b + 1))
                for t in range(ST):
                    for c in range(PAIRS):
                        last = product(pe, ps_aux[:, t * D:(t + 1) * D], tuple(o[:, c, t * P:(t + 1) * P] for o in OT),
                                       tuple(w[:, c * D:(c + 1) * D] for w in WO), c == 0 and t == 0, c == PAIRS - 1)
                last.then_inc(out_done, 1)

            def turn(b, first, last):
                for n in range(H):
                    for later, m, what, k in projections(n, last):
                        project(b + later, m, what, k)
                    for at in ahead(b, n + 2, last):
                        scores(*at)
                    transpose_probs(b, n)
                    if n:
                        attend(b, n - 1)
                    elif not first:
                        attend(b - 1, H - 1)
                    if n == OUT_AT and not first:
                        output(b - 1)
                    if n == TRANSPOSE_AT and not last:
                        pe.wait_ge(out_used, b + 1)
                        transposes(b + 1)

            pe.wait_ge(id_ready, 2)
            transposes(0)
            for m in range(AHEAD):
                project(0, m, *PJ[m][:2])
            scores(0, 0)
            scores(0, 1)
            turns(pe, turn)
            attend(B - 1, H - 1)
            output(B - 1)

        def vpad_half(vp, g, t, odd):
            return vp[:, g % 2, t, odd:HG:2, DH * odd:DH * odd + DH]

        def v_half(bank, t, odd):
            return bank[:, t * 256:(t + 1) * 256].rearrange("p (h d) -> p h d", d=DH)[:, odd:HG:2, :]

        @block.scalar
        def _(act):
            def hi_of_transposes(b):
                for i in range(NSRC):
                    act.wait_ge(tr_done, NSRC * b + i + 1)
                    act.activation(XT[i][0][:, :, :].rearrange("p c s -> p (c s)"), ps_aux[:, :], ACT.Copy).then_inc(tr_hi, 1)

            def hi_of_projection(b, m, what, k):
                act.wait_ge(pj_done, NPJ * b + m + 1)
                if what == "v":
                    wait(act, pv_done, H * b + HG * (k - 1))
                    for t in range(ST):
                        for odd in range(2):
                            last = act.activation(vpad_half(VP[0], k, t, odd), v_half(ps_pj[m % 2], t, odd), ACT.Copy)
                else:
                    wait(act, s_done, H * b + 2 * (k - 1))
                    last = act.activation(QK[0][:, k % 2, :, :].rearrange("p a s -> p (a s)"), ps_pj[m % 2][:, :], ACT.Copy)
                last.then_inc(pj_hi, 1)

            def exps(b, n):
                act.wait_ge(max_ready, H * b + n + 1)
                wait(act, t_done, H * b + n - 1)
                for t in range(ST):
                    last = act.activation(PR[:, n % 2, t, :], SM[:, n % 2, t, :], ACT.Exp,
                                          bias=nb[:, n % 2, t:t + 1], scale=SCALE, accum_out=sums[:, n % 2, t:t + 1])
                last.then_inc(exp_ready, 1)

            def hi_of_probs(b, n):
                act.wait_ge(t_done, H * b + n + 1)
                wait(act, pv_done, H * b + n - 1)
                act.activation(PT[0][:, n % 2, :, :].rearrange("p a s -> p (a s)"), ps_t[n % 2][:, :], ACT.Copy).then_inc(t_hi, 1)

            def hi_of_pair(b, pair):
                act.wait_ge(pv_done, H * b + 2 * pair + 2)
                if pair == 0:
                    wait(act, out_done, b)
                act.activation(OT[0][:, pair, :], ps_pv[:, 0:S], ACT.Copy).then_inc(o_hi, 1)

            def turn(b, first, last):
                for n in range(H):
                    for later, m, what, k in projections(n, last):
                        hi_of_projection(b + later, m, what, k)
                    hi_of_probs(b, n)
                    if n >= 2 and n % 2 == 0:
                        hi_of_pair(b, n // 2 - 1)
                    elif n == 0 and not first:
                        hi_of_pair(b - 1, PAIRS - 1)
                    for at in ahead(b, n + 2, last):
                        exps(*at)
                    if n == TRANSPOSE_AT and not last:
                        hi_of_transposes(b + 1)

            hi_of_transposes(0)
            act.wait_ge(pad_ready, 2)
            for m in range(AHEAD):
                hi_of_projection(0, m, *PJ[m][:2])
            exps(0, 0)
            exps(0, 1)
            turns(act, turn)
            hi_of_pair(B - 1, PAIRS - 1)

        @block.vector
        def _(dve):
            per_turn = 1 + 2 * H + 1 + norm_links(ST, True) + (0 if cross else norm_links(ST, False))

            def lo_of_transposes(b):
                for i in range(NSRC):
                    dve.wait_ge(tr_hi, NSRC * b + i + 1)
                    dve.tensor_tensor(XT[i][1][:, :, :].rearrange("p c s -> p (c s)"), ps_aux[:, :],
                                      XT[i][0][:, :, :].rearrange("p c s -> p (c s)").bitcast(F32),
                                      ALU.subtract).then_inc(tr_lo, 1)

            def prepare(link, b):
                dve.wait_ge(x_in[0], 16 * (b + 1))
                if not cross:
                    layer_norm(dve, link, dve_gate, xin[0][:, :, :], qrow, ywork, xin[0], statx, vepsx_ready,
                               rstdx_ready, b + 1)
                dve.sem_inc(qrow_ready, 1)

            def build_mask(link, b):
                link(dve.tensor_scalar(maskf[:, :], mask8[:, bass.ds(b * S, S)], MASKED, None, ALU.mult))

            def lo_of_projection(b, m, what, k):
                dve.wait_ge(pj_hi, NPJ * b + m + 1)
                if what == "v":
                    for t in range(ST):
                        for odd in range(2):
                            last = dve.tensor_tensor(vpad_half(VP[1], k, t, odd), v_half(ps_pj[m % 2], t, odd),
                                                     vpad_half(VP[0], k, t, odd).bitcast(F32), ALU.subtract)
                else:
                    last = dve.tensor_tensor(QK[1][:, k % 2, :, :].rearrange("p a s -> p (a s)"), ps_pj[m % 2][:, :],
                                             QK[0][:, k % 2, :, :].rearrange("p a s -> p (a s)").bitcast(F32),
                                             ALU.subtract)
                last.then_inc(pj_lo, 1)

            def masked_max(link, b, n):
                dve.wait_ge(s_done, H * b + n + 1)
                dve.sem_inc(dve_gate, 1)
                wait(dve, exp_ready, H * b + n - 1)
                dve.sem_inc(dve_gate, 1)
                for t in range(ST):
                    link.mark(dve.tensor_tensor_reduce(SM[:, n % 2, t, :], ps_s[n % 2][:, t * S:(t + 1) * S],
                                                       maskf[:, :], 1.0, LOWEST, ALU.add, ALU.max,
                                                       mx[:, n % 2, t:t + 1]))
                link.join()
                dve.tensor_scalar(nb[:, n % 2, :], mx[:, n % 2, :], -SCALE, None, ALU.mult).then_inc(max_ready, 1)

            def normalise(b, n):
                dve.wait_ge(exp_ready, H * b + n + 1)
                dve.sem_inc(dve_gate, 1)
                wait(dve, norm_ready, H * b + n - 1)
                dve.sem_inc(dve_gate, 1)
                dve.reciprocal(inv[:, n % 2, :], sums[:, n % 2, :]).then_inc(inv_ready, 1)
                dve.wait_ge(inv_ready, H * b + n + 1)
                for t in range(1, ST):
                    last = dve.tensor_scalar(PR[:, n % 2, t, :], PR[:, n % 2, t, :], inv[:, n % 2, t:t + 1], None, ALU.mult)
                last.then_inc(norm2_ready, 1)

            def lo_of_probs(b, n):
                dve.wait_ge(t_hi, H * b + n + 1)
                dve.tensor_tensor(PT[1][:, n % 2, :, :].rearrange("p a s -> p (a s)"), ps_t[n % 2][:, :],
                                  PT[0][:, n % 2, :, :].rearrange("p a s -> p (a s)").bitcast(F32),
                                  ALU.subtract).then_inc(t_lo, 1)

            def lo_of_pair(b, pair):
                dve.wait_ge(o_hi, PAIRS * b + pair + 1)
                dve.tensor_tensor(OT[1][:, pair, :], ps_pv[:, 0:S], OT[0][:, pair, :].bitcast(F32),
                                  ALU.subtract).then_inc(o_lo, 1)

            def residual_sum(link, b):
                dve.wait_ge(out_done, b + 1)
                dve.wait_ge(resid_ready, ST * (b + 1))
                link(dve.tensor_tensor(y[:, :, :].rearrange("p t d -> p (t d)"), ps_aux[:, :],
                                       resid[:, :, :].rearrange("p t d -> p (t d)"), ALU.add))
                dve.sem_inc(out_used, 1)

            def output_norm(link, b):
                layer_norm(dve, link, dve_gate, y[:, :, :], yout, ywork, y, stat, veps_ready, rstd_ready,
                           b + 1, g_b[:, :], beta_b[:, :])
                dve.sem_inc(y_ready, 1)

            def turn_with(link):
                def turn(b, first, last):
                    for n in range(H):
                        for later, m, what, k in projections(n, last):
                            lo_of_projection(b + later, m, what, k)
                        for at in ahead(b, n + 1, last):
                            normalise(*at)
                        lo_of_probs(b, n)
                        if n == H - 2 and not last:
                            build_mask(link, b + 1)
                        for at in ahead(b, n + 2, last):
                            masked_max(link, *at)
                        if n >= 2 and n % 2 == 0:
                            lo_of_pair(b, n // 2 - 1)
                        elif n == 0 and not first:
                            lo_of_pair(b - 1, PAIRS - 1)
                        if n == SUM_AT and not first:
                            residual_sum(link, b - 1)
                        if n == NORM_AT and not first:
                            output_norm(link, b - 1)
                        if n == PREPARE_AT and not last:
                            prepare(link, b + 1)
                        if n == TRANSPOSE_AT and not last:
                            lo_of_transposes(b + 1)
                return turn

            link = Links(dve, dve_links)
            prepare(link, 0)
            dve.wait_ge(const_in, 64)
            dve.sem_inc(out_used, 1)
            lo_of_transposes(0)
            dve.wait_ge(pad_ready, 2)
            build_mask(link, 0)
            for m in range(AHEAD):
                lo_of_projection(0, m, *PJ[m][:2])
            masked_max(link, 0, 0)
            masked_max(link, 0, 1)
            normalise(0, 0)
            turn_with(link)(0, True, False)
            before = link.n
            with dve.Fori(1, B - 1) as b:
                link = Links(dve, dve_links, per_turn, b - 1, before)
                turn_with(link)(b, False, False)
                link.close()
            link = Links(dve, dve_links, before=before + (B - 2) * per_turn)
            turn_with(link)(B - 1, False, True)
            lo_of_pair(B - 1, PAIRS - 1)
            residual_sum(link, B - 1)
            output_norm(link, B - 1)


def mlp(nc, name, x_rows, h_rows, fc1, fc1_b, fc2, fc2_b, g, beta, w1s, w2s, w3s, wg, logits, normed_rows,
        partial_rows, slot_rows):
    NT, N, BLOCKS = 4, 512, T // 512
    with ExitStack() as ctx:
        def sb(n, shape, dt=F32):
            return ctx.enter_context(nc.sbuf_tensor(f"{name}_{n}", shape, dt))

        def psum(n):
            return ctx.enter_context(nc.psum_tensor(f"{name}_{n}", [P, 512], F32))

        def sem(n):
            return ctx.enter_context(nc.semaphore(f"{name}_{n}"))

        def split(n, shape):
            return sb(n + "_hi", shape, F32R), sb(n + "_lo", shape, F32R)

        FC1, FC2, W1, W2, W3 = (split(n, [P, 2048]) for n in ("fc1", "fc2", "w1", "w2", "w3"))
        load_weights(nc, list(zip((fc1, fc2, w1s, w2s, w3s), (FC1, FC2, W1, W2, W3))), name)
        WG, wg_raw = split("wg", [P, KC * E]), sb("wg_raw", [P, KC, E])
        hin, xin = sb("hin", [P, NT, D]), sb("xin", [P, NT, D])
        XT = split("xt", [P, KC, N])
        GT = split("gt", [P, FC, N])
        G, A = sb("g", [P, 2, N]), sb("a", [P, 2, N])
        y, ywork, ynorm, squares = (sb(n, [P, NT, D]) for n in ("y", "ywork", "ynorm", "squares"))
        x2, xn2, part = (sb(n, [P, NT, D]) for n in ("x2", "xn2", "part"))
        b1, b2_b, g_b, beta_b = sb("b1", [P, FC]), sb("b2_b", [P, D]), sb("g_b", [P, D]), sb("beta_b", [P, D])
        ident, zeros, stat, mhalf = sb("ident", [P, P]), sb("zeros", [P, 768]), sb("stat", [P, 5, NT]), sb("mhalf", [P, NT])
        ps_u, ps_v, ps_d = ([psum(f"ps_{k}{i}") for i in range(2)] for k in "uvd")
        ps_l = psum("ps_l")

        const_in, wg_in, id_ready, half_ready = sem("const_in"), sem("wg_in"), sem("id_ready"), sem("half_ready")
        zero_ready, zeroed = sem("zero_ready"), sem("zeroed")
        h_in, x_in, rows_used = sem("h_in"), sem("x_in"), sem("rows_used")
        xn2_ready, part_ready, xn2_stored, part_stored = sem("xn2_ready"), sem("part_ready"), sem("xn2_stored"), sem("part_stored")
        tr_done, tr_hi, tr_lo = sem("tr_done"), sem("tr_hi"), sem("tr_lo")
        up_done, gelu_ready, act_lo = sem("up_done"), sem("gelu_ready"), sem("act_lo")
        down_done, logits_done, wg_ready = sem("down_done"), sem("logits_done"), sem("wg_ready")
        veps_ready, rstd_ready = sem("veps_ready"), sem("rstd_ready")
        dve_links, dve_gate, pool_gate = sem("dve_links"), sem("dve_gate"), sem("pool_gate")
        block = ctx.enter_context(nc.Block())

        @block.sync
        def _(sp):
            for dst, src in ((b2_b, fc2_b), (g_b, g), (beta_b, beta)):
                sp.dma_start(dst[:, :], src.partition_broadcast(P)).then_inc(const_in, 16)
            with nc.allow_non_contiguous_dma(reason="1024 biases, once"):
                sp.dma_start(b1[:, :], fc1_b.rearrange("(m p) -> p m", p=P)).then_inc(const_in, 16)
            sp.dma_start(wg_raw[:, :, :], wg.rearrange("(c p) e -> p c e", p=P)).then_inc(wg_in, 16)
            sp.wait_ge(zero_ready, 1)
            flat = slot_rows.rearrange("(n p r) d -> n p (r d)", p=P, r=3)
            for i in range(flat.shape[0]):
                sp.dma_start(flat[i], zeros[:, :]).then_inc(zeroed, 16)
            sp.wait_ge(zeroed, 16 * flat.shape[0])

        @block.gpsimd
        def _(pool):
            make_identity(pool, ident[:, :], id_ready)
            pool.memset(zeros[:, :], 0.0).then_inc(zero_ready, 1)
            pool.memset(mhalf[:, :], -0.5).then_inc(half_ready, 1)
            pool.wait_ge(half_ready, 1)

            def load(t):
                pool.dma_start(hin[:, :, :], h_rows(t)).then_inc(h_in, 16)
                pool.dma_start(xin[:, :, :], x_rows(t)).then_inc(x_in, 16)

            load(0)
            with pool.Fori(0, BLOCKS) as t:
                for k in range(2):
                    pool.wait_ge(veps_ready, 2 * t + k + 1)
                    pool.tensor_tensor(stat[:, 4, :], stat[:, 3, :], mhalf[:, :], ALU.pow).then_inc(rstd_ready, 1)
                    if k == 0:
                        pool.wait_ge(rows_used, t + 1)
                        pool.sem_inc(pool_gate, 1)
                        load(pool.snap((t + 1) % BLOCKS))
                pool.wait_ge(xn2_ready, t + 1)
                pool.sem_inc(pool_gate, 1)
                pool.dma_start(normed_rows(t), xn2[:, :, :]).then_inc(xn2_stored, 16)
                pool.wait_ge(part_ready, t + 2)
                pool.sem_inc(pool_gate, 1)
                pool.dma_start(partial_rows(t), part[:, :, :]).then_inc(part_stored, 16)
                pool.wait_ge(xn2_stored, 16 * (t + 1))
                pool.sem_inc(pool_gate, 1)
                pool.wait_ge(part_stored, 16 * (t + 1))
                pool.sem_inc(pool_gate, 1)
            pool.wait_ge(h_in, 16 * (BLOCKS + 1))
            pool.wait_ge(x_in, 16 * (BLOCKS + 1))

        @block.tensor
        def _(pe):
            pe.wait_ge(id_ready, 2)
            pe.wait_ge(wg_ready, 2)
            with pe.Fori(0, BLOCKS) as t:
                for k, (src, ups, down) in enumerate(((hin, ((FC1, ps_u),), FC2), (xn2, ((W1, ps_u), (W2, ps_v)), W3))):
                    if k == 0:
                        pe.wait_ge(h_in, 16 * (t + 1))
                        pe.wait_ge(part_ready, t + 1)
                    else:
                        pe.wait_ge(xn2_ready, t + 1)
                    for c in range(KC):
                        for i in range(NT):
                            last = pe.transpose(ps_d[c][:, i * P:(i + 1) * P], src[:, i, c * P:(c + 1) * P], ident[:, :])
                        last.then_inc(tr_done, 1)
                    pe.wait_ge(tr_lo, 2 * KC * t + KC * (k + 1))
                    if k:
                        for i in range(NT):
                            for c in range(KC):
                                last = product(pe, ps_l[:, i * E:(i + 1) * E], tuple(w[:, c, i * P:(i + 1) * P] for w in XT),
                                               tuple(w[:, c * E:(c + 1) * E] for w in WG), c == 0 and i == 0, c == KC - 1)
                        last.then_inc(logits_done, 1)
                    for m in range(FC):
                        if m >= 2:
                            pe.wait_ge(act_lo, 2 * FC * t + FC * k + m - 1)
                        for W, bank in ups:
                            for c in range(KC):
                                last = product(pe, bank[m % 2][:, :], tuple(w[:, c * FF + m * P:c * FF + (m + 1) * P] for w in W),
                                               tuple(w[:, c, :] for w in XT), c == 0, c == KC - 1)
                        last.then_inc(up_done, 1)
                    for m in range(FC):
                        pe.wait_ge(act_lo, 2 * FC * t + FC * k + m + 1)
                        for i in range(NT):
                            last = product(pe, ps_d[i // 2][:, (i % 2) * D:(i % 2 + 1) * D],
                                           tuple(w[:, m, i * P:(i + 1) * P] for w in GT),
                                           tuple(w[:, m * D:(m + 1) * D] for w in down), m == 0 and i % 2 == 0, m == FC - 1)
                    last.then_inc(down_done, 1)

        @block.scalar
        def _(act):
            act.wait_ge(const_in, 64)
            act.wait_ge(wg_in, 16)
            act.activation(WG[0][:, :], wg_raw[:, :, :].rearrange("p c e -> p (c e)"), ACT.Copy).then_inc(wg_ready, 1)
            with act.Fori(0, BLOCKS) as t:
                for k in range(2):
                    for c in range(KC):
                        act.wait_ge(tr_done, 2 * KC * t + KC * k + c + 1)
                        act.activation(XT[0][:, c, :], ps_d[c][:, :], ACT.Copy).then_inc(tr_hi, 1)
                    for m in range(FC):
                        act.wait_ge(up_done, 2 * FC * t + FC * k + m + 1)
                        if m >= 2:
                            act.wait_ge(act_lo, 2 * FC * t + FC * k + m - 1)
                        act.activation(G[:, m % 2, :], ps_u[m % 2][:, :], ACT.Gelu,
                                       bias=b1[:, m:m + 1] if k == 0 else 0.0).then_inc(gelu_ready, 1)

        @block.vector
        def _(dve):
            per_turn = FC + 2 + NT + norm_links(NT, True) + 1 + norm_links(NT, False) + 2 * FC + 1 + 2
            dve.wait_ge(wg_ready, 1)
            dve.tensor_tensor(WG[1][:, :], wg_raw[:, :, :].rearrange("p c e -> p (c e)"), WG[0][:, :].bitcast(F32),
                              ALU.subtract).then_inc(wg_ready, 1)
            dve.wait_ge(const_in, 64)
            dve.sem_inc(part_ready, 1)
            with dve.Fori(0, BLOCKS) as t:
                link = Links(dve, dve_links, per_turn, t)
                for k in range(2):
                    for c in range(KC):
                        dve.wait_ge(tr_hi, 2 * KC * t + KC * k + c + 1)
                        dve.tensor_tensor(XT[1][:, c, :], ps_d[c][:, :], XT[0][:, c, :].bitcast(F32), ALU.subtract).then_inc(tr_lo, 1)
                    if k:
                        dve.wait_ge(logits_done, t + 1)
                        link(dve.tensor_copy(logits[:, bass.ds(t * NT, NT), :].rearrange("p t e -> p (t e)"), ps_l[:, 0:NT * E]))
                    for m in range(FC):
                        act_in = G[:, m % 2, :]
                        dve.wait_ge(gelu_ready, 2 * FC * t + FC * k + m + 1)
                        if k:
                            dve.wait_ge(up_done, 2 * FC * t + FC * k + m + 1)
                            act_in = A[:, m % 2, :]
                            link(dve.tensor_tensor(act_in, ps_v[m % 2][:, :], G[:, m % 2, :], ALU.mult))
                        link(dve.tensor_copy(GT[0][:, m, :], act_in))
                        dve.tensor_tensor(GT[1][:, m, :], act_in, GT[0][:, m, :].bitcast(F32), ALU.subtract).then_inc(act_lo, 1)
                    dve.wait_ge(down_done, 2 * t + k + 1)
                    rows = (y, part)[k]
                    for i in range(2):
                        if k == 0 and i == 0:
                            dve.wait_ge(x_in, 16 * (t + 1))
                        link.mark(dve.tensor_tensor(rows[:, 2 * i:2 * i + 2, :].rearrange("p t d -> p (t d)"), ps_d[i][:, :],
                                                    (hin, x2)[k][:, 2 * i:2 * i + 2, :].rearrange("p t d -> p (t d)"), ALU.add))
                    link.join()
                    if k == 0:
                        for i in range(NT):
                            link.mark(dve.tensor_tensor(y[:, i, :], y[:, i, :], b2_b[:, :], ALU.add))
                        link.join()
                        layer_norm(dve, link, dve_gate, y[:, :, :], ynorm, ywork, squares, stat, veps_ready, rstd_ready,
                                   2 * t + 1, g_b[:, :], beta_b[:, :])
                        link(dve.tensor_tensor(x2[:, :, :].rearrange("p t d -> p (t d)"), xin[:, :, :].rearrange("p t d -> p (t d)"),
                                               ynorm[:, :, :].rearrange("p t d -> p (t d)"), ALU.add))
                        dve.sem_inc(rows_used, 1)
                        layer_norm(dve, link, dve_gate, x2[:, :, :], xn2, ywork, squares, stat, veps_ready, rstd_ready,
                                   2 * t + 2)
                        dve.sem_inc(xn2_ready, 1)
                    else:
                        dve.sem_inc(part_ready, 1)
                link.close()


def route(nc, logits, position, slot_expert, normed, slot_rows):
    with ExitStack() as ctx:
        def sb(n, shape, dt=F32):
            return ctx.enter_context(nc.sbuf_tensor(f"route_{n}", shape, dt))

        def sem(n):
            return ctx.enter_context(nc.semaphore(f"route_{n}"))

        rows = sb("rows", [P, TT, D])
        expert_no, slot_no, step_no = sb("expert_no", [P, TT, E]), sb("slot_no", [P, SLOTS, E]), sb("step_no", [P, E, T // SLOT])
        before, ones = sb("before", [P, P], BF16), sb("ones", [P, P], BF16)
        top, key, first = sb("top", [P, TT]), sb("key", [P, TT, E]), sb("first", [P, TT])
        chosen, chosen16 = sb("chosen", [P, TT, E]), sb("chosen16", [P, TT, E], BF16)
        of_tile, prefix, where = sb("of_tile", [P, TT, E]), sb("prefix", [P, TT + 1, E]), sb("where", [P, TT, E])
        steps, slots, first_slot = sb("steps", [P, E, T // SLOT]), sb("slots", [P, E]), sb("first_slot", [P, E + 1])
        ended, expert_f, pos_f = sb("ended", [P, SLOTS, E]), sb("expert_f", [P, SLOTS]), sb("pos_f", [P, TT])
        ps = [ctx.enter_context(nc.psum_tensor(f"route_ps{i}", [P, 512], F32)) for i in range(2)]
        rows_in, consts, pool_links, dve_links = sem("rows_in"), sem("consts"), sem("pool_links"), sem("dve_links")
        chosen_ready, counted, pos_ready, scattered = sem("chosen_ready"), sem("counted"), sem("pos_ready"), sem("scattered")
        block = ctx.enter_context(nc.Block())

        @block.sync
        def _(sp):
            sp.dma_start(rows[:, :, :], normed.rearrange("(t p) d -> p t d", p=P)).then_inc(rows_in, 16)

        @block.gpsimd
        def _(pool):
            kw = dict(allow_small_or_imprecise_dtypes=True)
            pool.iota(expert_no[:, :, :], [[0, TT], [1, E]], base=0, channel_multiplier=0, **kw).then_inc(consts, 1)
            pool.iota(slot_no[:, :, :], [[1, SLOTS], [0, E]], base=0, channel_multiplier=0, **kw).then_inc(consts, 1)
            pool.iota(step_no[:, :, :], [[0, E], [SLOT, T // SLOT]], base=0, channel_multiplier=0, **kw).then_inc(consts, 1)
            pool.memset(ones[:, :], 1.0).then_inc(consts, 1)
            pool.memset(before[:, :], 1.0).then_inc(pool_links, 1)
            pool.wait_ge(pool_links, 1)
            pool.affine_select(out=before[:, :], in_=before[:, :], compare_op=ALU.is_gt, fill=0.0, base=0,
                               pattern=[[1, P]], channel_multiplier=-1).then_inc(consts, 1)
            pool.wait_ge(rows_in, 16)
            pool.wait_ge(pos_ready, 1)
            for t in range(TT):
                pool.indirect_dma_start(slot_rows, bass.IndirectOffsetOnAxis(ap=position[:, t:t + 1], axis=0),
                                        rows[:, t, :], None).then_inc(scattered, 16)
            pool.wait_ge(scattered, 16 * TT)

        @block.tensor
        def _(pe):
            pe.wait_ge(consts, 5)
            pe.wait_ge(chosen_ready, 1)
            flat = chosen16[:, :, :].rearrange("p t e -> p (t e)")
            pe.matmul(ps[0][:, 0:TT * E], before[:, :], flat, start=True, stop=True)
            pe.matmul(ps[1][:, 0:TT * E], ones[:, :], flat, start=True, stop=True).then_inc(counted, 1)

        @block.vector
        def _(dve):
            link = Links(dve, dve_links)
            dve.wait_ge(consts, 5)
            over_e = lambda ap: ap.unsqueeze(2).to_broadcast([P, TT, E])
            link(dve.tensor_reduce(top[:, :], logits[:, :, :], AX.X, ALU.max))
            link(dve.tensor_tensor(key[:, :, :], logits[:, :, :], over_e(top[:, :]), ALU.is_equal))
            link(dve.scalar_tensor_tensor(out=key[:, :, :], in0=key[:, :, :], scalar=-float(E), in1=expert_no[:, :, :],
                                          op0=ALU.mult, op1=ALU.add))
            link(dve.tensor_reduce(first[:, :], key[:, :, :], AX.X, ALU.min))
            link(dve.tensor_tensor(chosen[:, :, :], key[:, :, :], over_e(first[:, :]), ALU.is_equal))
            dve.tensor_copy(chosen16[:, :, :], chosen[:, :, :]).then_inc(chosen_ready, 1)
            link(dve.memset(prefix[:, 0, :], 0.0))
            dve.wait_ge(counted, 1)
            link(dve.tensor_copy(of_tile[:, :, :].rearrange("p t e -> p (t e)"), ps[1][:, 0:TT * E]))
            for t in range(TT):
                link(dve.tensor_tensor(prefix[:, t + 1, :], prefix[:, t, :], of_tile[:, t, :], ALU.add))
            link(dve.tensor_tensor(steps[:, :, :], prefix[:, TT, :].unsqueeze(2).to_broadcast([P, E, T // SLOT]),
                                   step_no[:, :, :], ALU.is_gt))
            link(dve.tensor_reduce(slots[:, :], steps[:, :, :], AX.X, ALU.add))
            link(dve.memset(first_slot[:, 0:1], 0.0))
            for e in range(E):
                link(dve.tensor_tensor(first_slot[:, e + 1:e + 2], first_slot[:, e:e + 1], slots[:, e:e + 1], ALU.add))
            link(dve.tensor_tensor(ended[:, :, :], slot_no[:, :, :],
                                   first_slot[:, 1:E + 1].unsqueeze(1).to_broadcast([P, SLOTS, E]), ALU.is_ge))
            link(dve.tensor_reduce(expert_f[:, :], ended[:, :, :], AX.X, ALU.add))
            link(dve.tensor_scalar(slot_expert[:, :], expert_f[:, :], float(E - 1), None, ALU.min))
            link(dve.tensor_tensor(where[:, :, :].rearrange("p t e -> p (t e)"), ps[0][:, 0:TT * E],
                                   prefix[:, 0:TT, :].rearrange("p t e -> p (t e)"), ALU.add))
            link(dve.scalar_tensor_tensor(out=where[:, :, :], in0=first_slot[:, 0:E].unsqueeze(1).to_broadcast([P, TT, E]),
                                          scalar=float(SLOT), in1=where[:, :, :], op0=ALU.mult, op1=ALU.add))
            link(dve.tensor_tensor(where[:, :, :], where[:, :, :], chosen[:, :, :], ALU.mult))
            link(dve.tensor_reduce(pos_f[:, :], where[:, :, :], AX.X, ALU.add))
            dve.tensor_copy(position[:, :], pos_f[:, :]).then_inc(pos_ready, 1)


def experts(nc, slot_expert, w1, w2, w3, slot_rows, slot_out):
    with ExitStack() as ctx:
        def sb(n, shape, dt=F32):
            return ctx.enter_context(nc.sbuf_tensor(f"moe_{n}", shape, dt))

        def psum(n):
            return ctx.enter_context(nc.psum_tensor(f"moe_{n}", [P, 512], F32))

        def sem(n):
            return ctx.enter_context(nc.semaphore(f"moe_{n}"))

        NT = SLOT // P
        raw = sb("raw", [P, 3, 2048])
        WH, WL = sb("w_hi", [P, 3, 2048], F32R), sb("w_lo", [P, 3, 2048], F32R)
        xin, yout, ident = sb("xin", [P, NT, D]), sb("yout", [P, NT, D]), sb("ident", [P, P])
        XT = sb("xt_hi", [P, KC, SLOT], F32R), sb("xt_lo", [P, KC, SLOT], F32R)
        GT = sb("gt_hi", [P, FC, SLOT], F32R), sb("gt_lo", [P, FC, SLOT], F32R)
        G, A = sb("g", [P, 2, SLOT]), sb("a", [P, 2, SLOT])
        ps_u, ps_v, ps_d, ps_t = [psum(f"u{i}") for i in range(2)], [psum(f"v{i}") for i in range(2)], psum("d"), psum("t")
        raw_in = [sem(f"raw_in{i}") for i in range(3)]
        w_hi, w_lo = [sem(f"w_hi{i}") for i in range(3)], [sem(f"w_lo{i}") for i in range(3)]
        id_ready, x_in, tr_done, tr_hi, tr_lo = sem("id_ready"), sem("x_in"), sem("tr_done"), sem("tr_hi"), sem("tr_lo")
        up_done, gelu_ready, act_lo, down_done = sem("up_done"), sem("gelu_ready"), sem("act_lo"), sem("down_done")
        y_ready, y_stored, dve_links = sem("y_ready"), sem("y_stored"), sem("dve_links")
        sp_gate, pool_gate, yout_free = sem("sp_gate"), sem("pool_gate"), sem("yout_free")
        block = ctx.enter_context(nc.Block())
        srcs = (w1.rearrange("e (c p) n -> p e c n", p=P), w2.rearrange("e (c p) n -> p e c n", p=P),
                w3.rearrange("e (c p) n -> p e c n", p=P))

        @block.sync
        def _(sp):
            def load(slot):
                e = sp.value_load(slot_expert[0:1, bass.ds(slot, 1)], min_val=0, max_val=E - 1)
                for k in range(3):
                    n = srcs[k].shape[3]
                    sp.dma_start(raw[:, k, :].rearrange("p (o c n) -> p o c n", o=1, n=n), srcs[k][:, bass.ds(e, 1), :, :])\
                        .then_inc(raw_in[k], 16)

            load(0)
            with sp.Fori(1, SLOTS) as s:
                for k in range(3):
                    sp.wait_ge(w_lo[k], s)
                    sp.sem_inc(sp_gate, 1)
                load(s)

        @block.gpsimd
        def _(pool):
            make_identity(pool, ident[:, :], id_ready)

            def load(s):
                pool.dma_start(xin[:, :, :], slot_rows[bass.ds(s * SLOT, SLOT), :].rearrange("(t p) d -> p t d", p=P))\
                    .then_inc(x_in, 16)

            def lo_of_weights(k, at):
                pool.wait_ge(w_hi[k], at)
                pool.tensor_tensor(WL[:, k, :], raw[:, k, :], WH[:, k, :].bitcast(F32), ALU.subtract).then_inc(w_lo[k], 1)

            def store(s):
                pool.wait_ge(y_ready, s + 2)
                pool.sem_inc(pool_gate, 1)
                pool.dma_start(slot_out[bass.ds(s * SLOT, SLOT), :].rearrange("(t p) d -> p t d", p=P), yout[:, :, :])\
                    .then_inc(y_stored, 16)

            def wait_stored(s):
                pool.wait_ge(y_stored, 16 * (s + 1))
                pool.sem_inc(yout_free, 1)

            pool.sem_inc(yout_free, 1)
            load(0)
            lo_of_weights(1, 1)
            lo_of_weights(2, 1)
            with pool.Fori(0, SLOTS - 1) as s:
                pool.wait_ge(tr_done, s + 1)
                pool.sem_inc(pool_gate, 1)
                load(s + 1)
                lo_of_weights(1, s + 2)
                store(s)
                lo_of_weights(2, s + 2)
                wait_stored(s)
            pool.wait_ge(tr_done, SLOTS)
            load(0)
            store(SLOTS - 1)
            wait_stored(SLOTS - 1)
            pool.wait_ge(x_in, 16 * (SLOTS + 1))

        @block.tensor
        def _(pe):
            def transposes(at):
                pe.wait_ge(x_in, 16 * at)
                for c in range(KC):
                    for t in range(NT):
                        last = pe.transpose(ps_t[:, c * SLOT + t * P:c * SLOT + (t + 1) * P], xin[:, t, c * P:(c + 1) * P], ident[:, :])
                last.then_inc(tr_done, 1)

            pe.wait_ge(id_ready, 2)
            transposes(1)
            with pe.Fori(0, SLOTS) as s:
                pe.wait_ge(tr_lo, s + 1)
                pe.wait_ge(w_lo[0], s + 1)
                pe.wait_ge(w_lo[1], s + 1)
                for m in range(FC):
                    if m >= 2:
                        pe.wait_ge(act_lo, FC * s + m - 1)
                    for k, bank in ((0, ps_u), (1, ps_v)):
                        for c in range(KC):
                            last = product(pe, bank[m % 2][:, 0:SLOT],
                                           tuple(w[:, k, c * FF + m * P:c * FF + (m + 1) * P] for w in (WH, WL)),
                                           tuple(x[:, c, :] for x in XT), c == 0, c == KC - 1)
                    last.then_inc(up_done, 1)
                transposes(s + 2)
                pe.wait_ge(w_lo[2], s + 1)
                pe.wait_ge(y_ready, s + 1)
                for m in range(FC):
                    pe.wait_ge(act_lo, FC * s + m + 1)
                    for t in range(NT):
                        last = product(pe, ps_d[:, t * D:(t + 1) * D], tuple(w[:, m, t * P:(t + 1) * P] for w in GT),
                                       tuple(w[:, 2, m * D:(m + 1) * D] for w in (WH, WL)), m == 0 and t == 0, m == FC - 1)
                last.then_inc(down_done, 1)

        @block.scalar
        def _(act):
            def hi_of_weights(k, at):
                act.wait_ge(raw_in[k], 16 * at)
                act.activation(WH[:, k, :], raw[:, k, :], ACT.Copy).then_inc(w_hi[k], 1)

            def hi_of_transposes(at):
                act.wait_ge(tr_done, at)
                act.activation(XT[0][:, :, :].rearrange("p c s -> p (c s)"), ps_t[:, :], ACT.Copy).then_inc(tr_hi, 1)

            def gelus(s):
                for m in range(FC):
                    act.wait_ge(up_done, FC * s + m + 1)
                    if m >= 2:
                        act.wait_ge(act_lo, FC * s + m - 1)
                    act.activation(G[:, m % 2, :], ps_u[m % 2][:, 0:SLOT], ACT.Gelu).then_inc(gelu_ready, 1)

            hi_of_weights(0, 1)
            hi_of_weights(1, 1)
            hi_of_weights(2, 1)
            hi_of_transposes(1)
            with act.Fori(0, SLOTS - 1) as s:
                gelus(s)
                hi_of_transposes(s + 2)
                hi_of_weights(0, s + 2)
                hi_of_weights(1, s + 2)
                act.wait_ge(down_done, s + 1)
                hi_of_weights(2, s + 2)
            gelus(SLOTS - 1)
            hi_of_transposes(SLOTS + 1)

        @block.vector
        def _(dve):
            per_turn = 2 * FC

            def lo_of_weights(at):
                dve.wait_ge(w_hi[0], at)
                dve.tensor_tensor(WL[:, 0, :], raw[:, 0, :], WH[:, 0, :].bitcast(F32), ALU.subtract).then_inc(w_lo[0], 1)

            def lo_of_transposes(at):
                dve.wait_ge(tr_hi, at)
                dve.tensor_tensor(XT[1][:, :, :].rearrange("p c s -> p (c s)"), ps_t[:, :],
                                  XT[0][:, :, :].rearrange("p c s -> p (c s)").bitcast(F32), ALU.subtract).then_inc(tr_lo, 1)

            def hidden(s):
                link = Links(dve, dve_links, per_turn, s)
                for m in range(FC):
                    dve.wait_ge(gelu_ready, FC * s + m + 1)
                    dve.wait_ge(up_done, FC * s + m + 1)
                    link(dve.tensor_tensor(A[:, m % 2, :], ps_v[m % 2][:, 0:SLOT], G[:, m % 2, :], ALU.mult))
                    link(dve.tensor_copy(GT[0][:, m, :], A[:, m % 2, :]))
                    dve.tensor_tensor(GT[1][:, m, :], A[:, m % 2, :], GT[0][:, m, :].bitcast(F32), ALU.subtract).then_inc(act_lo, 1)
                link.close()

            def store(s):
                dve.wait_ge(down_done, s + 1)
                dve.wait_ge(yout_free, s + 1)
                dve.tensor_copy(yout[:, :, :].rearrange("p t d -> p (t d)"), ps_d[:, :]).then_inc(y_ready, 1)

            dve.sem_inc(y_ready, 1)
            lo_of_weights(1)
            lo_of_transposes(1)
            with dve.Fori(0, SLOTS - 1) as s:
                hidden(s)
                lo_of_transposes(s + 2)
                lo_of_weights(s + 2)
                store(s)
            hidden(SLOTS - 1)
            lo_of_transposes(SLOTS + 1)
            store(SLOTS - 1)


def combine(nc, position, partial, slot_out, out):
    with ExitStack() as ctx:
        part = ctx.enter_context(nc.sbuf_tensor("comb_part", [P, TT, D], F32))
        rows = ctx.enter_context(nc.sbuf_tensor("comb_rows", [P, TT, D], F32))
        part_in, summed, stored = (ctx.enter_context(nc.semaphore(f"comb_{n}")) for n in ("part_in", "summed", "stored"))
        gathered = [ctx.enter_context(nc.semaphore(f"comb_gathered{q}")) for q in range(TT // 4)]
        out_v = out.rearrange("(t p) d -> p t d", p=P)
        block = ctx.enter_context(nc.Block())

        @block.sync
        def _(sp):
            sp.dma_start(part[:, :, :], partial.rearrange("(t p) d -> p t d", p=P)).then_inc(part_in, 16)
            for q in range(0, TT, 4):
                sp.wait_ge(summed, q + 4)
                sp.dma_start(out_v[:, q:q + 4, :], part[:, q:q + 4, :]).then_inc(stored, 16)
            sp.wait_ge(stored, 16 * (TT // 4))

        @block.gpsimd
        def _(pool):
            for t in range(TT):
                pool.indirect_dma_start(rows[:, t, :], None, slot_out,
                                        bass.IndirectOffsetOnAxis(ap=position[:, t:t + 1], axis=0)).then_inc(gathered[t // 4], 16)

        @block.vector
        def _(dve):
            dve.wait_ge(part_in, 16)
            for t in range(TT):
                if t % 4 == 0:
                    dve.wait_ge(gathered[t // 4], 64)
                dve.tensor_tensor(part[:, t, :], part[:, t, :], rows[:, t, :], ALU.add).then_inc(summed, 1)


def rows_of_batch(x):
    return lambda b: x[bass.ds(b * S, S), :].rearrange("(t p) d -> p t d", p=P)


def rows_of_block(x):
    return lambda t: x[bass.ds(t * 512, 512), :].rearrange("(t p) d -> p t d", p=P)


def build(nc, a, out):
    flat = lambda ap: ap.rearrange("b s d -> (b s) d")
    xa = lambda n: a["L0_xattn_" + n]
    ff = lambda n: a["L0_ffn_" + n]
    scratch = lambda n, rows: nc.dram_tensor(n, (rows, D), F32, kind="Internal").ap()
    after_self, after_cross, normed, partial = (scratch(n, T) for n in ("after_self", "after_cross", "normed", "partial"))
    slot_rows, slot_out = scratch("slot_rows", SLOTS * SLOT), scratch("slot_out", SLOTS * SLOT)
    x, context, mask = flat(a["x"]), flat(a["ctx_1024"]), a["mask_BxS2_bk0"]
    attention(nc, "sa", False, rows_of_batch(x), None, mask, xa("sa_wq"), xa("sa_wk"), xa("sa_wv"), xa("sa_wo"),
              xa("sa_bo"), xa("ln1_g"), xa("ln1_b"), rows_of_batch(after_self))
    attention(nc, "ca", True, rows_of_batch(after_self), rows_of_batch(context), mask, xa("ca_wq"), xa("ca_wk"),
              xa("ca_wv"), xa("ca_wo"), xa("ca_bo"), xa("ln2_g"), xa("ln2_b"), rows_of_batch(after_cross))
    with (nc.sbuf_tensor("logits", [P, TT, E], F32) as logits, nc.sbuf_tensor("position", [P, TT], I32) as position,
          nc.sbuf_tensor("slot_expert", [P, SLOTS], I32) as slot_expert):
        mlp(nc, "mlp", rows_of_block(x), rows_of_block(after_cross), xa("fc1_w"), xa("fc1_b"), xa("fc2_w"), xa("fc2_b"),
            xa("ln3_g"), xa("ln3_b"), ff("w1s"), ff("w2s"), ff("w3s"), ff("Wg"), logits, rows_of_block(normed),
            rows_of_block(partial), slot_rows)
        route(nc, logits, position, slot_expert, normed, slot_rows)
        experts(nc, slot_expert, ff("W1"), ff("W2"), ff("W3"), slot_rows, slot_out)
        combine(nc, position, partial, slot_out, flat(out))


_OUTS = [((B, S, D), "float32")]


def kernel(**inputs):
    import numpy as _np
    import concourse.bacc as _bacc
    from concourse.bass_utils import run_bass_kernel_spmd as _run

    nc = _bacc.Bacc("TRN2", target_bir_lowering=False, num_devices=1)
    arrays, args = {}, {}
    for name, a in inputs.items():
        a = _np.ascontiguousarray(a)
        arrays[f"in_{name}"] = a
        args[name] = nc.dram_tensor(f"in_{name}", a.shape, mybir.dt.from_np(a.dtype), kind="ExternalInput").ap()
    outs = [nc.dram_tensor(f"out_{i}", shape, mybir.dt.from_np(_np.dtype(dt)), kind="ExternalOutput").ap()
            for i, (shape, dt) in enumerate(_OUTS)]
    build(nc, args, outs[0])
    r = _run(nc, [arrays], core_ids=[0])
    return r.results[0]["out_0"]
```

```python
from contextlib import ExitStack

import concourse.bass as bass
from concourse import mybir

F32 = mybir.dt.float32
F32R = mybir.dt.float32r
BF16 = mybir.dt.bfloat16
I32 = mybir.dt.int32
U8 = mybir.dt.uint8
ACT = mybir.ActivationFunctionType
ALU = mybir.AluOpType
AX = mybir.AxisListType

P = 128
B, S, D = 8, 256, 256
T = B * S
H, DH = 16, 64
INNER = H * DH
FF = 1024
E = 8
KC = D // P
ST = S // P
PAIRS = H // 2
GROUPS = 4
HG = H // GROUPS
FC = FF // P
EPS = 1e-5
SCALE = DH ** -0.5
MASKED = -(2.0 ** 126)
LOWEST = -3.0e38
SLOT = 256
SLOTS = T // SLOT + E - 1
TT = T // P


class Links:

    def __init__(self, eng, sem, per_turn=0, turn=0, before=0):
        self.eng, self.sem, self.per_turn, self.turn, self.before, self.n = eng, sem, per_turn, turn, before, 0

    def mark(self, ins):
        ins.then_inc(self.sem, 1)
        self.n += 1

    def join(self):
        self.eng.wait_ge(self.sem, self.turn * self.per_turn + (self.before + self.n))

    def __call__(self, ins):
        self.mark(ins)
        self.join()

    def close(self):
        assert self.n == self.per_turn, (self.n, self.per_turn)


def product(pe, out, stationary, moving, start, stop):
    (wh, wl), (mh, ml) = stationary, moving
    pe.matmul(out, wl, mh, start=start, stop=False, skip_group_check=True)
    pe.matmul(out, wh, ml, start=False, stop=False, skip_group_check=True)
    return pe.matmul(out, wh, mh, start=False, stop=stop, skip_group_check=True)


def make_identity(pool, ident, sem):
    pool.memset(ident, 0.0).then_inc(sem, 1)
    pool.wait_ge(sem, 1)
    pool.affine_select(out=ident, in_=ident, compare_op=ALU.not_equal, fill=1.0, base=0,
                       pattern=[[-1, P]], channel_multiplier=1).then_inc(sem, 1)


def layer_norm(dve, link, gate, x, out, work, squares, stat, veps_ready, rstd_ready, rstd_at, g=None, beta=None):
    n = x.shape[1]
    total, nmean, ssq, veps, rstd = (stat[:, k, 0:n] for k in range(5))
    link(dve.tensor_reduce(total, x, AX.X, ALU.add))
    link(dve.tensor_scalar(nmean, total, -1.0 / D, None, ALU.mult))
    for t in range(n):
        link.mark(dve.tensor_scalar(work[:, t, :], x[:, t, :], nmean[:, t:t + 1], None, ALU.add))
    for t in range(n):
        link.join()
        dve.sem_inc(gate, 1)
        link.mark(dve.tensor_tensor_reduce(squares[:, t, :], work[:, t, :], work[:, t, :], 1.0, 0.0,
                                           ALU.mult, ALU.add, ssq[:, t:t + 1]))
    link.join()
    dve.tensor_scalar(veps, ssq, 1.0 / D, EPS, ALU.mult, ALU.add).then_inc(veps_ready, 1)
    dve.wait_ge(rstd_ready, rstd_at)
    for t in range(n):
        if g is None:
            link.mark(dve.tensor_scalar(out[:, t, :], work[:, t, :], rstd[:, t:t + 1], None, ALU.mult))
        else:
            link.mark(dve.scalar_tensor_tensor(out=out[:, t, :], in0=work[:, t, :],
                                               scalar=rstd[:, t:t + 1], in1=g, op0=ALU.mult, op1=ALU.mult))
    if g is not None:
        link.join()
        for t in range(n):
            link.mark(dve.tensor_tensor(out[:, t, :], out[:, t, :], beta, ALU.add))
    link.join()


def norm_links(n, affine):
    return 2 + 3 * n + (n if affine else 0)


def load_weights(nc, weights, prefix):
    PIECE = 2048
    with ExitStack() as ctx:
        raw = [ctx.enter_context(nc.sbuf_tensor(f"{prefix}_raw{i}", [P, PIECE], F32)) for i in range(3)]
        landed = [ctx.enter_context(nc.semaphore(f"{prefix}_landed{i}")) for i in range(3)]
        hi_ready = ctx.enter_context(nc.semaphore(f"{prefix}_hi_ready"))
        lo_ready = ctx.enter_context(nc.semaphore(f"{prefix}_lo_ready"))
        pieces = []
        for w, (hi, lo) in weights:
            k, n = w.shape
            step = PIECE // n
            for c in range(0, k // P, step):
                pieces.append((w.rearrange("(c p) n -> p c n", p=P)[:, c:c + step, :], n,
                               hi[:, c * n:(c + step) * n], lo[:, c * n:(c + step) * n]))
        with nc.Block() as block:
            @block.sync
            def _(sp):
                for i, (src, n, _, _) in enumerate(pieces):
                    if i >= 3:
                        sp.wait_ge(lo_ready, i - 2)
                    sp.dma_start(raw[i % 3][:, :].rearrange("p (c n) -> p c n", n=n), src).then_inc(landed[i % 3], 16)

            @block.scalar
            def _(act):
                for i, (_, _, hi, _) in enumerate(pieces):
                    act.wait_ge(landed[i % 3], 16 * (i // 3 + 1))
                    act.activation(hi, raw[i % 3][:, :], ACT.Copy).then_inc(hi_ready, 1)

            @block.vector
            def _(dve):
                for i, (_, _, hi, lo) in enumerate(pieces):
                    dve.wait_ge(hi_ready, i + 1)
                    dve.tensor_tensor(lo, raw[i % 3][:, :], hi.bitcast(F32), ALU.subtract).then_inc(lo_ready, 1)


def attention(nc, name, cross, x_rows, ctx_rows, mask, wq, wk, wv, wo, bo, g, beta, out_rows):
    with ExitStack() as ctx:
        def sb(n, shape, dt=F32):
            return ctx.enter_context(nc.sbuf_tensor(f"{name}_{n}", shape, dt))

        def psum(n):
            return ctx.enter_context(nc.psum_tensor(f"{name}_{n}", [P, 512], F32))

        def sem(n):
            return ctx.enter_context(nc.semaphore(f"{name}_{n}"))

        def split(n, shape):
            return sb(n + "_hi", shape, F32R), sb(n + "_lo", shape, F32R)

        WQ, WK, WV, WO = (split(n, [P, KC * INNER]) for n in ("wq", "wk", "wv", "wo"))
        load_weights(nc, list(zip((wq, wk, wv, wo), (WQ, WK, WV, WO))), name)

        def wpart(W, c, a, b):
            return tuple(w[:, c * INNER + a:c * INNER + b] for w in W)

        NSRC = 2 if cross else 1
        xin = [sb(f"xin{i}", [P, ST, D]) for i in range(NSRC)]
        qrow = sb("qrow", [P, ST, D]) if not cross else xin[0]
        resid = sb("resid", [P, ST, D])
        XT = [split(f"xt{i}", [P, KC, S]) for i in range(NSRC)]
        QT, KVT = XT[0], XT[-1]
        VP = split("vpad", [P, 2, ST, HG, P])
        QK = split("qk", [P, 2, 2, S])
        SM = sb("scores", [P, 2, ST, S])
        PR = sb("probs", [P, 2, ST, S])
        PT = split("probs_t", [P, 2, ST, S])
        OT = split("heads_t", [P, PAIRS, S])
        y, ywork, yout = sb("y", [P, ST, D]), sb("ywork", [P, ST, D]), sb("yout", [P, ST, D])
        mask8, maskf = sb("mask8", [P, T], U8), sb("maskf", [P, S])
        bo_b, g_b, beta_b = sb("bo_b", [P, D]), sb("g_b", [P, D]), sb("beta_b", [P, D])
        ident = sb("ident", [P, P])
        mx, nb, sums, inv = (sb(n, [P, 2, ST]) for n in ("mx", "nb", "sums", "inv"))
        stat, statx = sb("stat", [P, 5, ST]), sb("statx", [P, 5, ST])
        mhalf = sb("mhalf", [P, ST])
        ps_pj = [psum(f"ps_pj{i}") for i in range(2)]
        ps_s = [psum(f"ps_s{i}") for i in range(2)]
        ps_t = [psum(f"ps_t{i}") for i in range(2)]
        ps_pv, ps_aux = psum("ps_pv"), psum("ps_aux")

        const_in, id_ready, pad_ready, half_ready = sem("const_in"), sem("id_ready"), sem("pad_ready"), sem("half_ready")
        x_in = [sem(f"x_in{i}") for i in range(NSRC)]
        y_stored, y_ready = sem("y_stored"), sem("y_ready")
        resid_ready, qrow_ready = sem("resid_ready"), sem("qrow_ready")
        tr_done, tr_hi, tr_lo = sem("tr_done"), sem("tr_hi"), sem("tr_lo")
        pj_done, pj_hi, pj_lo = sem("pj_done"), sem("pj_hi"), sem("pj_lo")
        s_done, max_ready, exp_ready, norm_ready = sem("s_done"), sem("max_ready"), sem("exp_ready"), sem("norm_ready")
        inv_ready, norm2_ready = sem("inv_ready"), sem("norm2_ready")
        t_done, t_hi, t_lo = sem("t_done"), sem("t_hi"), sem("t_lo")
        pv_done, o_hi, o_lo = sem("pv_done"), sem("o_hi"), sem("o_lo")
        out_done, out_used = sem("out_done"), sem("out_used")
        veps_ready, rstd_ready = sem("veps_ready"), sem("rstd_ready")
        vepsx_ready, rstdx_ready = sem("vepsx_ready"), sem("rstdx_ready")
        dve_links, dve_gate, pool_gate = sem("dve_links"), sem("dve_gate"), sem("pool_gate")

        NPJ = GROUPS + PAIRS
        PJ = [("qk", 0, H - 4), ("v", 0, H - 3), ("qk", 1, H - 2)]
        for n in range(H - 4):
            if n % 2 == 0 and n // 2 + 2 < PAIRS:
                PJ.append(("qk", n // 2 + 2, n))
            if n % HG == 1:
                PJ.append(("v", n // HG + 1, n))
        AHEAD = 3
        assert len(PJ) == NPJ
        OUT_AT, SUM_AT, RESID_AT, LOAD_AT, NORM_AT, STORE_AT, PREPARE_AT, TRANSPOSE_AT = 1, 5, 6, 6, 7, 8, 9, H - 5
        OUT_PARTS = 4

        def projections(step, last):
            return [(int(m < AHEAD), m, what, k) for m, (what, k, at) in enumerate(PJ)
                    if at == step and not (last and m < AHEAD)]

        def projected(what, k):
            return 1 + next(m for m, x in enumerate(PJ) if x[:2] == (what, k))

        def ahead(b, n, last):
            if n < H:
                return [(b, n)]
            return [] if last else [(b + 1, n - H)]

        def wait(eng, sem, value):
            if not (isinstance(value, int) and value <= 0):
                eng.wait_ge(sem, value)

        def turns(eng, turn):
            turn(0, True, False)
            with eng.Fori(1, B - 1) as b:
                turn(b, False, False)
            turn(B - 1, False, True)

        block = ctx.enter_context(nc.Block())

        @block.sync
        def _(sp):
            for dst, src in ((bo_b, bo), (g_b, g), (beta_b, beta)):
                sp.dma_start(dst[:, :], src.partition_broadcast(P)).then_inc(const_in, 16)
            sp.dma_start(mask8[:, :], mask.rearrange("b s -> (b s)").partition_broadcast(P)).then_inc(const_in, 16)

        @block.gpsimd
        def _(pool):
            make_identity(pool, ident[:, :], id_ready)
            pool.memset(mhalf[:, :], -0.5).then_inc(half_ready, 1)
            for vp in VP:
                pool.memset(vp[:, :, :, :, :].rearrange("p a b c d -> p (a b c d)").bitcast(F32), 0.0).then_inc(pad_ready, 1)
            pool.wait_ge(half_ready, 1)

            def load(b):
                for i, src in enumerate((x_rows, ctx_rows)[:NSRC]):
                    pool.dma_start(xin[i][:, :, :], src(b)).then_inc(x_in[i], 16)

            def power(st, ready, done, at):
                pool.wait_ge(ready, at)
                pool.tensor_tensor(st[:, 4, :], st[:, 3, :], mhalf[:, :], ALU.pow).then_inc(done, 1)

            def normalise(b, n):
                pool.wait_ge(inv_ready, H * b + n + 1)
                pool.sem_inc(pool_gate, 1)
                pool.tensor_scalar(PR[:, n % 2, 0, :], PR[:, n % 2, 0, :], inv[:, n % 2, 0:1], None, ALU.mult)\
                    .then_inc(norm_ready, 1)

            def store(b):
                pool.wait_ge(y_ready, b + 1)
                pool.sem_inc(pool_gate, 1)
                pool.dma_start(out_rows(b), yout[:, :, :]).then_inc(y_stored, 16)

            def turn(b, first, last):
                for n in range(H):
                    for at in ahead(b, n + 1, last):
                        normalise(*at)
                    if n == RESID_AT:
                        pool.wait_ge(qrow_ready, b + 1)
                        pool.wait_ge(out_used, b + 1)
                        for t in range(ST):
                            pool.tensor_tensor(resid[:, t, :], qrow[:, t, :], bo_b[:, :], ALU.add).then_inc(resid_ready, 1)
                    if n == LOAD_AT and not last:
                        pool.wait_ge(resid_ready, ST * (b + 1))
                        pool.wait_ge(tr_done, NSRC * (b + 1))
                        pool.sem_inc(pool_gate, 1)
                        load(b + 1)
                    if n == NORM_AT and not first:
                        power(stat, veps_ready, rstd_ready, b)
                    if n == STORE_AT and not first:
                        store(b - 1)
                    if n == PREPARE_AT and not cross and not last:
                        power(statx, vepsx_ready, rstdx_ready, b + 2)
                    if n == H - 2 and not first:
                        pool.wait_ge(y_stored, 16 * b)
                        pool.sem_inc(pool_gate, 1)

            load(0)
            if not cross:
                power(statx, vepsx_ready, rstdx_ready, 1)
            pool.wait_ge(const_in, 64)
            normalise(0, 0)
            turns(pool, turn)
            power(stat, veps_ready, rstd_ready, B)
            store(B - 1)
            pool.wait_ge(y_stored, 16 * B)

        @block.tensor
        def _(pe):
            def transposes(b):
                for i in range(NSRC):
                    if cross:
                        pe.wait_ge(x_in[i], 16 * (b + 1))
                    else:
                        pe.wait_ge(qrow_ready, b + 1)
                    if i:
                        pe.wait_ge(tr_lo, NSRC * b + i)
                    src = (qrow if i == 0 else xin[i])
                    for c in range(KC):
                        for t in range(ST):
                            last = pe.transpose(ps_aux[:, c * S + t * P:c * S + (t + 1) * P],
                                                src[:, t, c * P:(c + 1) * P], ident[:, :])
                    last.then_inc(tr_done, 1)

            def project(b, m, what, k):
                bank = ps_pj[m % 2]
                pe.wait_ge(tr_lo, NSRC * (b + 1))
                wait(pe, pj_lo, NPJ * b + m - 1)
                if what == "v":
                    for t in range(ST):
                        for c in range(KC):
                            last = product(pe, bank[:, t * 256:(t + 1) * 256],
                                           tuple(w[:, c, t * P:(t + 1) * P] for w in KVT),
                                           wpart(WV, c, k * 256, (k + 1) * 256), c == 0 and t == 0, c == KC - 1)
                else:
                    for j, (W, X) in enumerate(((WQ, QT), (WK, KVT))):
                        for c in range(KC):
                            last = product(pe, bank[:, j * S:(j + 1) * S], wpart(W, c, k * P, (k + 1) * P),
                                           tuple(x[:, c, :] for x in X), c == 0 and j == 0, c == KC - 1)
                last.then_inc(pj_done, 1)

            def scores(b, n):
                pair, r = n // 2, DH * (n % 2)
                pe.wait_ge(pj_lo, NPJ * b + projected("qk", pair))
                wait(pe, max_ready, H * b + n - 1)
                for t in range(ST):
                    last = product(pe, ps_s[n % 2][:, t * S:(t + 1) * S],
                                   tuple(w[r:r + DH, pair % 2, 0, t * P:(t + 1) * P] for w in QK),
                                   tuple(w[r:r + DH, pair % 2, 1, :] for w in QK), t == 0, t == ST - 1)
                last.then_inc(s_done, 1)

            def transpose_probs(b, n):
                pe.wait_ge(norm_ready, H * b + n + 1)
                pe.wait_ge(norm2_ready, H * b + n + 1)
                wait(pe, t_lo, H * b + n - 1)
                for j in range(ST):
                    for t in range(ST):
                        last = pe.transpose(ps_t[n % 2][:, j * S + t * P:j * S + (t + 1) * P],
                                            PR[:, n % 2, t, j * P:(j + 1) * P], ident[:, :])
                last.then_inc(t_done, 1)

            def attend(b, n):
                pe.wait_ge(t_lo, H * b + n + 1)
                if n % HG == 0:
                    pe.wait_ge(pj_lo, NPJ * b + projected("v", n // HG))
                if n % 2 == 0:
                    wait(pe, o_lo, PAIRS * b + n // 2)
                for j in range(ST):
                    last = product(pe, ps_pv[:, 0:S], tuple(v[:, n // HG % 2, j, n % HG, :] for v in VP),
                                   tuple(p[:, n % 2, j, :] for p in PT),
                                   n % 2 == 0 and j == 0, n % 2 == 1 and j == ST - 1)
                last.then_inc(pv_done, 1)

            def output(b, part):
                if part == 0:
                    pe.wait_ge(o_lo, PAIRS * (b + 1))
                for c in range(part * PAIRS // OUT_PARTS, (part + 1) * PAIRS // OUT_PARTS):
                    for t in range(ST):
                        last = product(pe, ps_aux[:, t * D:(t + 1) * D], tuple(o[:, c, t * P:(t + 1) * P] for o in OT),
                                       tuple(w[:, c * D:(c + 1) * D] for w in WO), c == 0 and t == 0, c == PAIRS - 1)
                last.then_inc(out_done, 1)

            def turn(b, first, last):
                for n in range(H):
                    for at in ahead(b, n + 2, last):
                        scores(*at)
                    transpose_probs(b, n)
                    if n:
                        attend(b, n - 1)
                    elif not first:
                        attend(b - 1, H - 1)
                    for later, m, what, k in projections(n, last):
                        project(b + later, m, what, k)
                    if 0 <= n - OUT_AT < OUT_PARTS and not first:
                        output(b - 1, n - OUT_AT)
                    if n == TRANSPOSE_AT and not last:
                        pe.wait_ge(out_used, b + 1)
                        transposes(b + 1)

            pe.wait_ge(id_ready, 2)
            transposes(0)
            for m in range(AHEAD):
                project(0, m, *PJ[m][:2])
            scores(0, 0)
            scores(0, 1)
            turns(pe, turn)
            attend(B - 1, H - 1)
            for part in range(OUT_PARTS):
                output(B - 1, part)

        def vpad_half(vp, g, t, odd):
            return vp[:, g % 2, t, odd:HG:2, DH * odd:DH * odd + DH]

        def v_half(bank, t, odd):
            return bank[:, t * 256:(t + 1) * 256].rearrange("p (h d) -> p h d", d=DH)[:, odd:HG:2, :]

        @block.scalar
        def _(act):
            def hi_of_transposes(b):
                for i in range(NSRC):
                    act.wait_ge(tr_done, NSRC * b + i + 1)
                    act.activation(XT[i][0][:, :, :].rearrange("p c s -> p (c s)"), ps_aux[:, :], ACT.Copy).then_inc(tr_hi, 1)

            def hi_of_projection(b, m, what, k):
                act.wait_ge(pj_done, NPJ * b + m + 1)
                if what == "v":
                    wait(act, pv_done, H * b + HG * (k - 1))
                    for t in range(ST):
                        for odd in range(2):
                            last = act.activation(vpad_half(VP[0], k, t, odd), v_half(ps_pj[m % 2], t, odd), ACT.Copy)
                else:
                    wait(act, s_done, H * b + 2 * (k - 1))
                    last = act.activation(QK[0][:, k % 2, :, :].rearrange("p a s -> p (a s)"), ps_pj[m % 2][:, :], ACT.Copy)
                last.then_inc(pj_hi, 1)

            def exps(b, n):
                act.wait_ge(max_ready, H * b + n + 1)
                wait(act, t_done, H * b + n - 1)
                for t in range(ST):
                    last = act.activation(PR[:, n % 2, t, :], SM[:, n % 2, t, :], ACT.Exp,
                                          bias=nb[:, n % 2, t:t + 1], scale=SCALE, accum_out=sums[:, n % 2, t:t + 1])
                last.then_inc(exp_ready, 1)

            def hi_of_probs(b, n):
                act.wait_ge(t_done, H * b + n + 1)
                wait(act, pv_done, H * b + n - 1)
                act.activation(PT[0][:, n % 2, :, :].rearrange("p a s -> p (a s)"), ps_t[n % 2][:, :], ACT.Copy).then_inc(t_hi, 1)

            def hi_of_pair(b, pair):
                act.wait_ge(pv_done, H * b + 2 * pair + 2)
                if pair * OUT_PARTS % PAIRS == 0:
                    wait(act, out_done, OUT_PARTS * (b - 1) + pair * OUT_PARTS // PAIRS + 1)
                act.activation(OT[0][:, pair, :], ps_pv[:, 0:S], ACT.Copy).then_inc(o_hi, 1)

            def turn(b, first, last):
                for n in range(H):
                    hi_of_probs(b, n)
                    if n >= 2 and n % 2 == 0:
                        hi_of_pair(b, n // 2 - 1)
                    elif n == 0 and not first:
                        hi_of_pair(b - 1, PAIRS - 1)
                    for at in ahead(b, n + 2, last):
                        exps(*at)
                    for later, m, what, k in projections(n, last):
                        hi_of_projection(b + later, m, what, k)
                    if n == TRANSPOSE_AT and not last:
                        hi_of_transposes(b + 1)

            hi_of_transposes(0)
            act.wait_ge(pad_ready, 2)
            for m in range(AHEAD):
                hi_of_projection(0, m, *PJ[m][:2])
            exps(0, 0)
            exps(0, 1)
            turns(act, turn)
            hi_of_pair(B - 1, PAIRS - 1)

        @block.vector
        def _(dve):
            per_turn = 1 + 2 * H + 1 + norm_links(ST, True) + (0 if cross else norm_links(ST, False))

            def lo_of_transposes(b):
                for i in range(NSRC):
                    dve.wait_ge(tr_hi, NSRC * b + i + 1)
                    dve.tensor_tensor(XT[i][1][:, :, :].rearrange("p c s -> p (c s)"), ps_aux[:, :],
                                      XT[i][0][:, :, :].rearrange("p c s -> p (c s)").bitcast(F32),
                                      ALU.subtract).then_inc(tr_lo, 1)

            def prepare(link, b):
                dve.wait_ge(x_in[0], 16 * (b + 1))
                if not cross:
                    layer_norm(dve, link, dve_gate, xin[0][:, :, :], qrow, ywork, xin[0], statx, vepsx_ready,
                               rstdx_ready, b + 1)
                dve.sem_inc(qrow_ready, 1)

            def build_mask(link, b):
                link(dve.tensor_scalar(maskf[:, :], mask8[:, bass.ds(b * S, S)], MASKED, None, ALU.mult))

            def lo_of_projection(b, m, what, k):
                dve.wait_ge(pj_hi, NPJ * b + m + 1)
                if what == "v":
                    for t in range(ST):
                        for odd in range(2):
                            last = dve.tensor_tensor(vpad_half(VP[1], k, t, odd), v_half(ps_pj[m % 2], t, odd),
                                                     vpad_half(VP[0], k, t, odd).bitcast(F32), ALU.subtract)
                else:
                    last = dve.tensor_tensor(QK[1][:, k % 2, :, :].rearrange("p a s -> p (a s)"), ps_pj[m % 2][:, :],
                                             QK[0][:, k % 2, :, :].rearrange("p a s -> p (a s)").bitcast(F32),
                                             ALU.subtract)
                last.then_inc(pj_lo, 1)

            def masked_max(link, b, n):
                dve.wait_ge(s_done, H * b + n + 1)
                dve.sem_inc(dve_gate, 1)
                wait(dve, exp_ready, H * b + n - 1)
                dve.sem_inc(dve_gate, 1)
                for t in range(ST):
                    link.mark(dve.tensor_tensor_reduce(SM[:, n % 2, t, :], ps_s[n % 2][:, t * S:(t + 1) * S],
                                                       maskf[:, :], 1.0, LOWEST, ALU.add, ALU.max,
                                                       mx[:, n % 2, t:t + 1]))
                link.join()
                dve.tensor_scalar(nb[:, n % 2, :], mx[:, n % 2, :], -SCALE, None, ALU.mult).then_inc(max_ready, 1)

            def normalise(b, n):
                dve.wait_ge(exp_ready, H * b + n + 1)
                dve.sem_inc(dve_gate, 1)
                wait(dve, norm_ready, H * b + n - 1)
                dve.sem_inc(dve_gate, 1)
                dve.reciprocal(inv[:, n % 2, :], sums[:, n % 2, :]).then_inc(inv_ready, 1)
                dve.wait_ge(inv_ready, H * b + n + 1)
                for t in range(1, ST):
                    last = dve.tensor_scalar(PR[:, n % 2, t, :], PR[:, n % 2, t, :], inv[:, n % 2, t:t + 1], None, ALU.mult)
                last.then_inc(norm2_ready, 1)

            def lo_of_probs(b, n):
                dve.wait_ge(t_hi, H * b + n + 1)
                dve.tensor_tensor(PT[1][:, n % 2, :, :].rearrange("p a s -> p (a s)"), ps_t[n % 2][:, :],
                                  PT[0][:, n % 2, :, :].rearrange("p a s -> p (a s)").bitcast(F32),
                                  ALU.subtract).then_inc(t_lo, 1)

            def lo_of_pair(b, pair):
                dve.wait_ge(o_hi, PAIRS * b + pair + 1)
                dve.tensor_tensor(OT[1][:, pair, :], ps_pv[:, 0:S], OT[0][:, pair, :].bitcast(F32),
                                  ALU.subtract).then_inc(o_lo, 1)

            def residual_sum(link, b):
                dve.wait_ge(out_done, OUT_PARTS * (b + 1))
                dve.wait_ge(resid_ready, ST * (b + 1))
                link(dve.tensor_tensor(y[:, :, :].rearrange("p t d -> p (t d)"), ps_aux[:, :],
                                       resid[:, :, :].rearrange("p t d -> p (t d)"), ALU.add))
                dve.sem_inc(out_used, 1)

            def output_norm(link, b):
                layer_norm(dve, link, dve_gate, y[:, :, :], yout, ywork, y, stat, veps_ready, rstd_ready,
                           b + 1, g_b[:, :], beta_b[:, :])
                dve.sem_inc(y_ready, 1)

            def turn_with(link):
                def turn(b, first, last):
                    for n in range(H):
                        if n == H - 2 and not last:
                            build_mask(link, b + 1)
                        for at in ahead(b, n + 2, last):
                            masked_max(link, *at)
                        for later, m, what, k in projections(n - 1, last):
                            lo_of_projection(b + later, m, what, k)
                        for at in ahead(b, n + 1, last):
                            normalise(*at)
                        lo_of_probs(b, n)
                        if n >= 2 and n % 2 == 0:
                            lo_of_pair(b, n // 2 - 1)
                        elif n == 0 and not first:
                            lo_of_pair(b - 1, PAIRS - 1)
                        if n == SUM_AT and not first:
                            residual_sum(link, b - 1)
                        if n == NORM_AT and not first:
                            output_norm(link, b - 1)
                        if n == PREPARE_AT and not last:
                            prepare(link, b + 1)
                        if n == TRANSPOSE_AT and not last:
                            lo_of_transposes(b + 1)
                return turn

            link = Links(dve, dve_links)
            prepare(link, 0)
            dve.wait_ge(const_in, 64)
            dve.sem_inc(out_used, 1)
            lo_of_transposes(0)
            dve.wait_ge(pad_ready, 2)
            build_mask(link, 0)
            for m in range(AHEAD):
                lo_of_projection(0, m, *PJ[m][:2])
            masked_max(link, 0, 0)
            masked_max(link, 0, 1)
            normalise(0, 0)
            turn_with(link)(0, True, False)
            before = link.n
            with dve.Fori(1, B - 1) as b:
                link = Links(dve, dve_links, per_turn, b - 1, before)
                turn_with(link)(b, False, False)
                link.close()
            link = Links(dve, dve_links, before=before + (B - 2) * per_turn)
            turn_with(link)(B - 1, False, True)
            lo_of_pair(B - 1, PAIRS - 1)
            residual_sum(link, B - 1)
            output_norm(link, B - 1)


def mlp(nc, name, x_rows, h_rows, fc1, fc1_b, fc2, fc2_b, g, beta, w1s, w2s, w3s, wg, logits, normed_rows,
        partial_rows, slot_rows):
    NT, N, BLOCKS = 4, 512, T // 512
    with ExitStack() as ctx:
        def sb(n, shape, dt=F32):
            return ctx.enter_context(nc.sbuf_tensor(f"{name}_{n}", shape, dt))

        def psum(n):
            return ctx.enter_context(nc.psum_tensor(f"{name}_{n}", [P, 512], F32))

        def sem(n):
            return ctx.enter_context(nc.semaphore(f"{name}_{n}"))

        def split(n, shape):
            return sb(n + "_hi", shape, F32R), sb(n + "_lo", shape, F32R)

        FC1, FC2, W1, W2, W3 = (split(n, [P, 2048]) for n in ("fc1", "fc2", "w1", "w2", "w3"))
        load_weights(nc, list(zip((fc1, fc2, w1s, w2s, w3s), (FC1, FC2, W1, W2, W3))), name)
        WG, wg_raw = split("wg", [P, KC * E]), sb("wg_raw", [P, KC, E])
        hin, xin = sb("hin", [P, NT, D]), sb("xin", [P, NT, D])
        XT = split("xt", [P, KC, N])
        GT = split("gt", [P, FC, N])
        G, A = sb("g", [P, 2, N]), sb("a", [P, 2, N])
        y, ywork, ynorm, squares = (sb(n, [P, NT, D]) for n in ("y", "ywork", "ynorm", "squares"))
        x2, xn2, part = (sb(n, [P, NT, D]) for n in ("x2", "xn2", "part"))
        b1, b2_b, g_b, beta_b = sb("b1", [P, FC]), sb("b2_b", [P, D]), sb("g_b", [P, D]), sb("beta_b", [P, D])
        ident, zeros, stat, mhalf = sb("ident", [P, P]), sb("zeros", [P, 768]), sb("stat", [P, 5, NT]), sb("mhalf", [P, NT])
        ps_u, ps_v, ps_d = ([psum(f"ps_{k}{i}") for i in range(2)] for k in "uvd")
        ps_l = psum("ps_l")

        const_in, wg_in, id_ready, half_ready = sem("const_in"), sem("wg_in"), sem("id_ready"), sem("half_ready")
        zero_ready, zeroed = sem("zero_ready"), sem("zeroed")
        h_in, x_in, rows_used = sem("h_in"), sem("x_in"), sem("rows_used")
        xn2_ready, part_ready, xn2_stored, part_stored = sem("xn2_ready"), sem("part_ready"), sem("xn2_stored"), sem("part_stored")
        tr_done, tr_hi, tr_lo = sem("tr_done"), sem("tr_hi"), sem("tr_lo")
        up_done, gelu_ready, gated, act_hi, act_lo = (sem(n) for n in ("up_done", "gelu_ready", "gated", "act_hi", "act_lo"))
        down_done, logits_done, wg_ready = sem("down_done"), sem("logits_done"), sem("wg_ready")
        veps_ready, rstd_ready = sem("veps_ready"), sem("rstd_ready")
        dve_links, dve_gate, pool_gate = sem("dve_links"), sem("dve_gate"), sem("pool_gate")
        block = ctx.enter_context(nc.Block())

        @block.sync
        def _(sp):
            for dst, src in ((b2_b, fc2_b), (g_b, g), (beta_b, beta)):
                sp.dma_start(dst[:, :], src.partition_broadcast(P)).then_inc(const_in, 16)
            with nc.allow_non_contiguous_dma(reason="1024 biases, once"):
                sp.dma_start(b1[:, :], fc1_b.rearrange("(m p) -> p m", p=P)).then_inc(const_in, 16)
            sp.dma_start(wg_raw[:, :, :], wg.rearrange("(c p) e -> p c e", p=P)).then_inc(wg_in, 16)
            sp.wait_ge(zero_ready, 1)
            flat = slot_rows.rearrange("(n p r) d -> n p (r d)", p=P, r=3)
            for i in range(flat.shape[0]):
                sp.dma_start(flat[i], zeros[:, :]).then_inc(zeroed, 16)
            sp.wait_ge(zeroed, 16 * flat.shape[0])

        @block.gpsimd
        def _(pool):
            make_identity(pool, ident[:, :], id_ready)
            pool.memset(zeros[:, :], 0.0).then_inc(zero_ready, 1)
            pool.memset(mhalf[:, :], -0.5).then_inc(half_ready, 1)
            pool.wait_ge(half_ready, 1)

            def load(t):
                pool.dma_start(hin[:, :, :], h_rows(t)).then_inc(h_in, 16)
                pool.dma_start(xin[:, :, :], x_rows(t)).then_inc(x_in, 16)

            load(0)
            with pool.Fori(0, BLOCKS) as t:
                for k in range(2):
                    pool.wait_ge(veps_ready, 2 * t + k + 1)
                    pool.tensor_tensor(stat[:, 4, :], stat[:, 3, :], mhalf[:, :], ALU.pow).then_inc(rstd_ready, 1)
                    if k == 0:
                        pool.wait_ge(rows_used, t + 1)
                        pool.sem_inc(pool_gate, 1)
                        load(pool.snap((t + 1) % BLOCKS))
                pool.wait_ge(xn2_ready, t + 1)
                pool.sem_inc(pool_gate, 1)
                pool.dma_start(normed_rows(t), xn2[:, :, :]).then_inc(xn2_stored, 16)
                pool.wait_ge(part_ready, t + 2)
                pool.sem_inc(pool_gate, 1)
                pool.dma_start(partial_rows(t), part[:, :, :]).then_inc(part_stored, 16)
                pool.wait_ge(xn2_stored, 16 * (t + 1))
                pool.sem_inc(pool_gate, 1)
                pool.wait_ge(part_stored, 16 * (t + 1))
                pool.sem_inc(pool_gate, 1)
            pool.wait_ge(h_in, 16 * (BLOCKS + 1))
            pool.wait_ge(x_in, 16 * (BLOCKS + 1))

        @block.tensor
        def _(pe):
            pe.wait_ge(id_ready, 2)
            pe.wait_ge(wg_ready, 2)
            with pe.Fori(0, BLOCKS) as t:
                for k, (src, ups, down) in enumerate(((hin, ((FC1, ps_u),), FC2), (xn2, ((W1, ps_u), (W2, ps_v)), W3))):
                    if k == 0:
                        pe.wait_ge(h_in, 16 * (t + 1))
                        pe.wait_ge(part_ready, t + 1)
                    else:
                        pe.wait_ge(xn2_ready, t + 1)
                    for c in range(KC):
                        for i in range(NT):
                            last = pe.transpose(ps_d[c][:, i * P:(i + 1) * P], src[:, i, c * P:(c + 1) * P], ident[:, :])
                        last.then_inc(tr_done, 1)
                    pe.wait_ge(tr_lo, 2 * KC * t + KC * (k + 1))
                    if k:
                        for i in range(NT):
                            for c in range(KC):
                                last = product(pe, ps_l[:, i * E:(i + 1) * E], tuple(w[:, c, i * P:(i + 1) * P] for w in XT),
                                               tuple(w[:, c * E:(c + 1) * E] for w in WG), c == 0 and i == 0, c == KC - 1)
                        last.then_inc(logits_done, 1)
                    for m in range(FC):
                        if m >= 2:
                            pe.wait_ge(gelu_ready, 2 * FC * t + FC * k + m - 1)
                            if k:
                                pe.wait_ge(gated, FC * t + m - 1)
                        for W, bank in ups:
                            for c in range(KC):
                                last = product(pe, bank[m % 2][:, :], tuple(w[:, c * FF + m * P:c * FF + (m + 1) * P] for w in W),
                                               tuple(w[:, c, :] for w in XT), c == 0, c == KC - 1)
                        last.then_inc(up_done, 1)
                    for m in range(FC):
                        pe.wait_ge(act_lo, 2 * FC * t + FC * k + m + 1)
                        for i in range(NT):
                            last = product(pe, ps_d[i // 2][:, (i % 2) * D:(i % 2 + 1) * D],
                                           tuple(w[:, m, i * P:(i + 1) * P] for w in GT),
                                           tuple(w[:, m * D:(m + 1) * D] for w in down), m == 0 and i % 2 == 0, m == FC - 1)
                    last.then_inc(down_done, 1)

        @block.scalar
        def _(act):
            act.wait_ge(const_in, 64)
            act.wait_ge(wg_in, 16)
            act.activation(WG[0][:, :], wg_raw[:, :, :].rearrange("p c e -> p (c e)"), ACT.Copy).then_inc(wg_ready, 1)
            with act.Fori(0, BLOCKS) as t:
                for k in range(2):
                    for c in range(KC):
                        act.wait_ge(tr_done, 2 * KC * t + KC * k + c + 1)
                        act.activation(XT[0][:, c, :], ps_d[c][:, :], ACT.Copy).then_inc(tr_hi, 1)

                    def hi_of_hidden(m):
                        if k:
                            act.wait_ge(gated, FC * t + m + 1)
                        else:
                            act.wait_ge(gelu_ready, 2 * FC * t + m + 1)
                        act.activation(GT[0][:, m, :], (G, A)[k][:, m % 2, :], ACT.Copy).then_inc(act_hi, 1)

                    for m in range(FC):
                        act.wait_ge(up_done, 2 * FC * t + FC * k + m + 1)
                        if m >= 2:
                            if k:
                                act.wait_ge(gated, FC * t + m - 1)
                            else:
                                act.wait_ge(act_lo, 2 * FC * t + m - 1)
                        act.activation(G[:, m % 2, :], ps_u[m % 2][:, :], ACT.Gelu,
                                       bias=b1[:, m:m + 1] if k == 0 else 0.0).then_inc(gelu_ready, 1)
                        if m >= 1:
                            hi_of_hidden(m - 1)
                    hi_of_hidden(FC - 1)

        @block.vector
        def _(dve):
            per_turn = 2 + NT + norm_links(NT, True) + 1 + norm_links(NT, False) + 1 + 2
            dve.wait_ge(wg_ready, 1)
            dve.tensor_tensor(WG[1][:, :], wg_raw[:, :, :].rearrange("p c e -> p (c e)"), WG[0][:, :].bitcast(F32),
                              ALU.subtract).then_inc(wg_ready, 1)
            dve.wait_ge(const_in, 64)
            dve.sem_inc(part_ready, 1)
            with dve.Fori(0, BLOCKS) as t:
                link = Links(dve, dve_links, per_turn, t)
                for k in range(2):
                    for c in range(KC):
                        dve.wait_ge(tr_hi, 2 * KC * t + KC * k + c + 1)
                        dve.tensor_tensor(XT[1][:, c, :], ps_d[c][:, :], XT[0][:, c, :].bitcast(F32), ALU.subtract).then_inc(tr_lo, 1)
                    if k:
                        dve.wait_ge(logits_done, t + 1)
                        link(dve.tensor_copy(logits[:, bass.ds(t * NT, NT), :].rearrange("p t e -> p (t e)"), ps_l[:, 0:NT * E]))

                    def lo_of_hidden(m):
                        dve.wait_ge(act_hi, 2 * FC * t + FC * k + m + 1)
                        dve.tensor_tensor(GT[1][:, m, :], (G, A)[k][:, m % 2, :], GT[0][:, m, :].bitcast(F32),
                                          ALU.subtract).then_inc(act_lo, 1)

                    for m in range(FC):
                        if k:
                            dve.wait_ge(gelu_ready, 2 * FC * t + FC * k + m + 1)
                            dve.wait_ge(up_done, 2 * FC * t + FC * k + m + 1)
                            if m >= 2:
                                dve.wait_ge(act_lo, 2 * FC * t + FC * k + m - 1)
                            dve.tensor_tensor(A[:, m % 2, :], ps_v[m % 2][:, :], G[:, m % 2, :], ALU.mult).then_inc(gated, 1)
                        if m >= 1:
                            lo_of_hidden(m - 1)
                    lo_of_hidden(FC - 1)
                    dve.wait_ge(down_done, 2 * t + k + 1)
                    rows = (y, part)[k]
                    for i in range(2):
                        if k == 0 and i == 0:
                            dve.wait_ge(x_in, 16 * (t + 1))
                        link.mark(dve.tensor_tensor(rows[:, 2 * i:2 * i + 2, :].rearrange("p t d -> p (t d)"), ps_d[i][:, :],
                                                    (hin, x2)[k][:, 2 * i:2 * i + 2, :].rearrange("p t d -> p (t d)"), ALU.add))
                    link.join()
                    if k == 0:
                        for i in range(NT):
                            link.mark(dve.tensor_tensor(y[:, i, :], y[:, i, :], b2_b[:, :], ALU.add))
                        link.join()
                        layer_norm(dve, link, dve_gate, y[:, :, :], ynorm, ywork, squares, stat, veps_ready, rstd_ready,
                                   2 * t + 1, g_b[:, :], beta_b[:, :])
                        link(dve.tensor_tensor(x2[:, :, :].rearrange("p t d -> p (t d)"), xin[:, :, :].rearrange("p t d -> p (t d)"),
                                               ynorm[:, :, :].rearrange("p t d -> p (t d)"), ALU.add))
                        dve.sem_inc(rows_used, 1)
                        layer_norm(dve, link, dve_gate, x2[:, :, :], xn2, ywork, squares, stat, veps_ready, rstd_ready,
                                   2 * t + 2)
                        dve.sem_inc(xn2_ready, 1)
                    else:
                        dve.sem_inc(part_ready, 1)
                link.close()


def route(nc, logits, position, slot_expert, normed, slot_rows):
    with ExitStack() as ctx:
        def sb(n, shape, dt=F32):
            return ctx.enter_context(nc.sbuf_tensor(f"route_{n}", shape, dt))

        def sem(n):
            return ctx.enter_context(nc.semaphore(f"route_{n}"))

        rows = sb("rows", [P, TT, D])
        expert_no, slot_no, step_no = sb("expert_no", [P, TT, E]), sb("slot_no", [P, SLOTS, E]), sb("step_no", [P, E, T // SLOT])
        before, ones = sb("before", [P, P], BF16), sb("ones", [P, P], BF16)
        top, key, first = sb("top", [P, TT]), sb("key", [P, TT, E]), sb("first", [P, TT])
        chosen, chosen16 = sb("chosen", [P, TT, E]), sb("chosen16", [P, TT, E], BF16)
        of_tile, prefix, where = sb("of_tile", [P, TT, E]), sb("prefix", [P, TT + 1, E]), sb("where", [P, TT, E])
        steps, slots, first_slot = sb("steps", [P, E, T // SLOT]), sb("slots", [P, E]), sb("first_slot", [P, E + 1])
        ended, expert_f, pos_f = sb("ended", [P, SLOTS, E]), sb("expert_f", [P, SLOTS]), sb("pos_f", [P, TT])
        ps = [ctx.enter_context(nc.psum_tensor(f"route_ps{i}", [P, 512], F32)) for i in range(2)]
        rows_in, consts, pool_links, dve_links = sem("rows_in"), sem("consts"), sem("pool_links"), sem("dve_links")
        chosen_ready, counted, pos_ready, scattered = sem("chosen_ready"), sem("counted"), sem("pos_ready"), sem("scattered")
        block = ctx.enter_context(nc.Block())

        @block.sync
        def _(sp):
            sp.dma_start(rows[:, :, :], normed.rearrange("(t p) d -> p t d", p=P)).then_inc(rows_in, 16)

        @block.gpsimd
        def _(pool):
            kw = dict(allow_small_or_imprecise_dtypes=True)
            pool.iota(expert_no[:, :, :], [[0, TT], [1, E]], base=0, channel_multiplier=0, **kw).then_inc(consts, 1)
            pool.iota(slot_no[:, :, :], [[1, SLOTS], [0, E]], base=0, channel_multiplier=0, **kw).then_inc(consts, 1)
            pool.iota(step_no[:, :, :], [[0, E], [SLOT, T // SLOT]], base=0, channel_multiplier=0, **kw).then_inc(consts, 1)
            pool.memset(ones[:, :], 1.0).then_inc(consts, 1)
            pool.memset(before[:, :], 1.0).then_inc(pool_links, 1)
            pool.wait_ge(pool_links, 1)
            pool.affine_select(out=before[:, :], in_=before[:, :], compare_op=ALU.is_gt, fill=0.0, base=0,
                               pattern=[[1, P]], channel_multiplier=-1).then_inc(consts, 1)
            pool.wait_ge(rows_in, 16)
            pool.wait_ge(pos_ready, 1)
            for t in range(TT):
                pool.indirect_dma_start(slot_rows, bass.IndirectOffsetOnAxis(ap=position[:, t:t + 1], axis=0),
                                        rows[:, t, :], None).then_inc(scattered, 16)
            pool.wait_ge(scattered, 16 * TT)

        @block.tensor
        def _(pe):
            pe.wait_ge(consts, 5)
            pe.wait_ge(chosen_ready, 1)
            flat = chosen16[:, :, :].rearrange("p t e -> p (t e)")
            pe.matmul(ps[0][:, 0:TT * E], before[:, :], flat, start=True, stop=True)
            pe.matmul(ps[1][:, 0:TT * E], ones[:, :], flat, start=True, stop=True).then_inc(counted, 1)

        @block.vector
        def _(dve):
            link = Links(dve, dve_links)
            dve.wait_ge(consts, 5)
            over_e = lambda ap: ap.unsqueeze(2).to_broadcast([P, TT, E])
            link(dve.tensor_reduce(top[:, :], logits[:, :, :], AX.X, ALU.max))
            link(dve.tensor_tensor(key[:, :, :], logits[:, :, :], over_e(top[:, :]), ALU.is_equal))
            link(dve.scalar_tensor_tensor(out=key[:, :, :], in0=key[:, :, :], scalar=-float(E), in1=expert_no[:, :, :],
                                          op0=ALU.mult, op1=ALU.add))
            link(dve.tensor_reduce(first[:, :], key[:, :, :], AX.X, ALU.min))
            link(dve.tensor_tensor(chosen[:, :, :], key[:, :, :], over_e(first[:, :]), ALU.is_equal))
            dve.tensor_copy(chosen16[:, :, :], chosen[:, :, :]).then_inc(chosen_ready, 1)
            link(dve.memset(prefix[:, 0, :], 0.0))
            dve.wait_ge(counted, 1)
            link(dve.tensor_copy(of_tile[:, :, :].rearrange("p t e -> p (t e)"), ps[1][:, 0:TT * E]))
            for t in range(TT):
                link(dve.tensor_tensor(prefix[:, t + 1, :], prefix[:, t, :], of_tile[:, t, :], ALU.add))
            link(dve.tensor_tensor(steps[:, :, :], prefix[:, TT, :].unsqueeze(2).to_broadcast([P, E, T // SLOT]),
                                   step_no[:, :, :], ALU.is_gt))
            link(dve.tensor_reduce(slots[:, :], steps[:, :, :], AX.X, ALU.add))
            link(dve.memset(first_slot[:, 0:1], 0.0))
            for e in range(E):
                link(dve.tensor_tensor(first_slot[:, e + 1:e + 2], first_slot[:, e:e + 1], slots[:, e:e + 1], ALU.add))
            link(dve.tensor_tensor(ended[:, :, :], slot_no[:, :, :],
                                   first_slot[:, 1:E + 1].unsqueeze(1).to_broadcast([P, SLOTS, E]), ALU.is_ge))
            link(dve.tensor_reduce(expert_f[:, :], ended[:, :, :], AX.X, ALU.add))
            link(dve.tensor_scalar(slot_expert[:, :], expert_f[:, :], float(E - 1), None, ALU.min))
            link(dve.tensor_tensor(where[:, :, :].rearrange("p t e -> p (t e)"), ps[0][:, 0:TT * E],
                                   prefix[:, 0:TT, :].rearrange("p t e -> p (t e)"), ALU.add))
            link(dve.scalar_tensor_tensor(out=where[:, :, :], in0=first_slot[:, 0:E].unsqueeze(1).to_broadcast([P, TT, E]),
                                          scalar=float(SLOT), in1=where[:, :, :], op0=ALU.mult, op1=ALU.add))
            link(dve.tensor_tensor(where[:, :, :], where[:, :, :], chosen[:, :, :], ALU.mult))
            link(dve.tensor_reduce(pos_f[:, :], where[:, :, :], AX.X, ALU.add))
            dve.tensor_copy(position[:, :], pos_f[:, :]).then_inc(pos_ready, 1)


def experts(nc, slot_expert, w1, w2, w3, slot_rows, slot_out):
    with ExitStack() as ctx:
        def sb(n, shape, dt=F32):
            return ctx.enter_context(nc.sbuf_tensor(f"moe_{n}", shape, dt))

        def psum(n):
            return ctx.enter_context(nc.psum_tensor(f"moe_{n}", [P, 512], F32))

        def sem(n):
            return ctx.enter_context(nc.semaphore(f"moe_{n}"))

        NT = SLOT // P
        COLS = KC * FF
        PIECES = 8
        PIECE = 3 * COLS // PIECES
        raw = sb("raw", [P, 3 * COLS])
        WH, WL = sb("w_hi", [P, 2, 3 * COLS], F32R), sb("w_lo", [P, 2, 3 * COLS], F32R)
        xin, yout, ident = sb("xin", [P, NT, D]), sb("yout", [P, NT, D]), sb("ident", [P, P])
        XT = sb("xt_hi", [P, KC, SLOT], F32R), sb("xt_lo", [P, KC, SLOT], F32R)
        GT = sb("gt_hi", [P, FC, SLOT], F32R), sb("gt_lo", [P, FC, SLOT], F32R)
        G, A = sb("g", [P, 2, SLOT]), sb("a", [P, 2, SLOT])
        ps_u, ps_v, ps_d, ps_t = [psum(f"u{i}") for i in range(3)], [psum(f"v{i}") for i in range(3)], psum("d"), psum("t")
        raw_in = [sem(f"raw_in{i}") for i in range(3)]
        w_hi, even_lo, odd_lo = sem("w_hi"), sem("even_lo"), sem("odd_lo")
        id_ready, x_in, tr_done, tr_hi, tr_lo = sem("id_ready"), sem("x_in"), sem("tr_done"), sem("tr_hi"), sem("tr_lo")
        up_done, gelu_ready, gated, act_hi, act_lo, down_done = (
            sem(n) for n in ("up_done", "gelu_ready", "gated", "act_hi", "act_lo", "down_done"))
        y_ready, y_stored = sem("y_ready"), sem("y_stored")
        sp_gate, pool_gate, yout_free = sem("sp_gate"), sem("pool_gate"), sem("yout_free")
        block = ctx.enter_context(nc.Block())
        srcs = (w1.rearrange("e (c p) n -> p e c n", p=P), w2.rearrange("e (c p) n -> p e c n", p=P),
                w3.rearrange("e (c p) n -> p e c n", p=P))

        assert SLOTS % 2 == 1

        def weight(buf, k, a, b):
            return tuple(w[:, buf, k * COLS + a:k * COLS + b] for w in (WH, WL))

        def piece_lo(eng, s, buf, i, done):
            cols = slice(i * PIECE, (i + 1) * PIECE)
            eng.wait_ge(w_hi, PIECES * s + i + 1)
            eng.tensor_tensor(WL[:, buf, cols], raw[:, cols], WH[:, buf, cols].bitcast(F32), ALU.subtract).then_inc(done, 1)

        def turns(eng, turn):
            with eng.Fori(0, SLOTS // 2) as i:
                turn(2 * i, 0, False)
                turn(2 * i + 1, 1, False)
            turn(SLOTS - 1, 0, True)

        @block.sync
        def _(sp):
            def load(slot, split=None):
                e = sp.value_load(slot_expert[0:1, bass.ds(slot, 1)], min_val=0, max_val=E - 1)
                for k in range(3):
                    n = srcs[k].shape[3]
                    if split is not None:
                        pieces = -(-(k + 1) * COLS // PIECE)
                        sp.wait_ge(even_lo, split * (PIECES // 2) + (pieces + 1) // 2)
                        sp.sem_inc(sp_gate, 1)
                        sp.wait_ge(odd_lo, split * (PIECES // 2) + pieces // 2)
                        sp.sem_inc(sp_gate, 1)
                    sp.dma_start(raw[:, k * COLS:(k + 1) * COLS].rearrange("p (o c n) -> p o c n", o=1, n=n), srcs[k][:, bass.ds(e, 1), :, :])\
                        .then_inc(raw_in[k], 16)

            load(0)
            with sp.Fori(1, SLOTS) as s:
                load(s, s - 1)

        @block.gpsimd
        def _(pool):
            make_identity(pool, ident[:, :], id_ready)

            def load(s):
                pool.dma_start(xin[:, :, :], slot_rows[bass.ds(s * SLOT, SLOT), :].rearrange("(t p) d -> p t d", p=P))\
                    .then_inc(x_in, 16)

            def store(s):
                pool.wait_ge(y_ready, s + 2)
                pool.sem_inc(pool_gate, 1)
                pool.dma_start(slot_out[bass.ds(s * SLOT, SLOT), :].rearrange("(t p) d -> p t d", p=P), yout[:, :, :])\
                    .then_inc(y_stored, 16)

            def wait_stored(s):
                pool.wait_ge(y_stored, 16 * (s + 1))
                pool.sem_inc(yout_free, 1)

            pool.sem_inc(yout_free, 1)
            load(0)
            for i in range(1, PIECES, 2):
                piece_lo(pool, 0, 0, i, odd_lo)

            def turn(s, buf, last):
                if not last:
                    pool.wait_ge(tr_done, s + 1)
                    pool.sem_inc(pool_gate, 1)
                    load(s + 1)
                    for i in range(1, PIECES, 2):
                        piece_lo(pool, s + 1, 1 - buf, i, odd_lo)
                store(s)
                wait_stored(s)

            turns(pool, turn)

        @block.tensor
        def _(pe):
            def transposes(at):
                pe.wait_ge(x_in, 16 * at)
                for c in range(KC):
                    for t in range(NT):
                        last = pe.transpose(ps_t[:, c * SLOT + t * P:c * SLOT + (t + 1) * P], xin[:, t, c * P:(c + 1) * P], ident[:, :])
                last.then_inc(tr_done, 1)

            pe.wait_ge(id_ready, 2)
            transposes(1)

            def turn(s, buf, last):
                pe.wait_ge(tr_lo, s + 1)
                pe.wait_ge(even_lo, PIECES // 2 * (s + 1))
                pe.wait_ge(odd_lo, PIECES // 2 * (s + 1))
                for m in range(FC):
                    if m >= 3:
                        pe.wait_ge(gated, FC * s + m - 2)
                    for k, bank in ((0, ps_u), (1, ps_v)):
                        for c in range(KC):
                            done = product(pe, bank[m % 3][:, 0:SLOT], weight(buf, k, c * FF + m * P, c * FF + (m + 1) * P),
                                           tuple(x[:, c, :] for x in XT), c == 0, c == KC - 1)
                    done.then_inc(up_done, 1)
                if not last:
                    transposes(s + 2)
                pe.wait_ge(y_ready, s + 1)
                for m in range(FC):
                    pe.wait_ge(act_lo, FC * s + m + 1)
                    for t in range(NT):
                        done = product(pe, ps_d[:, t * D:(t + 1) * D], tuple(w[:, m, t * P:(t + 1) * P] for w in GT),
                                       weight(buf, 2, m * D, (m + 1) * D), m == 0 and t == 0, m == FC - 1)
                done.then_inc(down_done, 1)

            turns(pe, turn)

        @block.scalar
        def _(act):
            def piece_hi(s, buf, i):
                for k in range(3):
                    if i == k * COLS // PIECE:
                        act.wait_ge(raw_in[k], 16 * (s + 1))
                cols = slice(i * PIECE, (i + 1) * PIECE)
                act.activation(WH[:, buf, cols], raw[:, cols], ACT.Copy).then_inc(w_hi, 1)

            def hi_of_transposes(at):
                act.wait_ge(tr_done, at)
                act.activation(XT[0][:, :, :].rearrange("p c s -> p (c s)"), ps_t[:, :], ACT.Copy).then_inc(tr_hi, 1)

            def hi_of_hidden(s, m):
                act.wait_ge(gated, FC * s + m + 1)
                act.activation(GT[0][:, m, :], A[:, m % 2, :], ACT.Copy).then_inc(act_hi, 1)

            def turn(s, buf, last):
                for m in range(FC):
                    act.wait_ge(up_done, FC * s + m + 1)
                    if m >= 2:
                        act.wait_ge(gated, FC * s + m - 1)
                    act.activation(G[:, m % 2, :], ps_u[m % 3][:, 0:SLOT], ACT.Gelu).then_inc(gelu_ready, 1)
                    if m >= 1:
                        hi_of_hidden(s, m - 1)
                    if not last:
                        piece_hi(s + 1, 1 - buf, m)
                hi_of_hidden(s, FC - 1)
                if not last:
                    hi_of_transposes(s + 2)

            for i in range(PIECES):
                piece_hi(0, 0, i)
            hi_of_transposes(1)
            turns(act, turn)

        @block.vector
        def _(dve):
            def lo_of_transposes(at):
                dve.wait_ge(tr_hi, at)
                dve.tensor_tensor(XT[1][:, :, :].rearrange("p c s -> p (c s)"), ps_t[:, :],
                                  XT[0][:, :, :].rearrange("p c s -> p (c s)").bitcast(F32), ALU.subtract).then_inc(tr_lo, 1)

            def turn(s, buf, last):
                def lo_of_hidden(m):
                    dve.wait_ge(act_hi, FC * s + m + 1)
                    dve.tensor_tensor(GT[1][:, m, :], A[:, m % 2, :], GT[0][:, m, :].bitcast(F32), ALU.subtract).then_inc(act_lo, 1)

                for m in range(FC):
                    dve.wait_ge(gelu_ready, FC * s + m + 1)
                    dve.wait_ge(up_done, FC * s + m + 1)
                    if m >= 2:
                        dve.wait_ge(act_lo, FC * s + m - 1)
                    dve.tensor_tensor(A[:, m % 2, :], ps_v[m % 3][:, 0:SLOT], G[:, m % 2, :], ALU.mult).then_inc(gated, 1)
                    if m >= 1:
                        lo_of_hidden(m - 1)
                    if m % 2 == 1 and not last:
                        piece_lo(dve, s + 1, 1 - buf, m - 1, even_lo)
                lo_of_hidden(FC - 1)
                if not last:
                    lo_of_transposes(s + 2)
                store(s)

            def store(s):
                dve.wait_ge(down_done, s + 1)
                dve.wait_ge(yout_free, s + 1)
                dve.tensor_copy(yout[:, :, :].rearrange("p t d -> p (t d)"), ps_d[:, :]).then_inc(y_ready, 1)

            dve.sem_inc(y_ready, 1)
            for i in range(0, PIECES, 2):
                piece_lo(dve, 0, 0, i, even_lo)
            lo_of_transposes(1)
            turns(dve, turn)


def combine(nc, position, partial, slot_out, out):
    with ExitStack() as ctx:
        part = ctx.enter_context(nc.sbuf_tensor("comb_part", [P, TT, D], F32))
        rows = ctx.enter_context(nc.sbuf_tensor("comb_rows", [P, TT, D], F32))
        part_in, summed, stored = (ctx.enter_context(nc.semaphore(f"comb_{n}")) for n in ("part_in", "summed", "stored"))
        gathered = [ctx.enter_context(nc.semaphore(f"comb_gathered{q}")) for q in range(TT // 4)]
        out_v = out.rearrange("(t p) d -> p t d", p=P)
        block = ctx.enter_context(nc.Block())

        @block.sync
        def _(sp):
            sp.dma_start(part[:, :, :], partial.rearrange("(t p) d -> p t d", p=P)).then_inc(part_in, 16)
            for q in range(0, TT, 4):
                sp.wait_ge(summed, q + 4)
                sp.dma_start(out_v[:, q:q + 4, :], part[:, q:q + 4, :]).then_inc(stored, 16)
            sp.wait_ge(stored, 16 * (TT // 4))

        @block.gpsimd
        def _(pool):
            for t in range(TT):
                pool.indirect_dma_start(rows[:, t, :], None, slot_out,
                                        bass.IndirectOffsetOnAxis(ap=position[:, t:t + 1], axis=0)).then_inc(gathered[t // 4], 16)

        @block.vector
        def _(dve):
            dve.wait_ge(part_in, 16)
            for t in range(TT):
                if t % 4 == 0:
                    dve.wait_ge(gathered[t // 4], 64)
                dve.tensor_tensor(part[:, t, :], part[:, t, :], rows[:, t, :], ALU.add).then_inc(summed, 1)


def rows_of_batch(x):
    return lambda b: x[bass.ds(b * S, S), :].rearrange("(t p) d -> p t d", p=P)


def rows_of_block(x):
    return lambda t: x[bass.ds(t * 512, 512), :].rearrange("(t p) d -> p t d", p=P)


def build(nc, a, out):
    flat = lambda ap: ap.rearrange("b s d -> (b s) d")
    xa = lambda n: a["L0_xattn_" + n]
    ff = lambda n: a["L0_ffn_" + n]
    scratch = lambda n, rows: nc.dram_tensor(n, (rows, D), F32, kind="Internal").ap()
    after_self, after_cross, normed, partial = (scratch(n, T) for n in ("after_self", "after_cross", "normed", "partial"))
    slot_rows, slot_out = scratch("slot_rows", SLOTS * SLOT), scratch("slot_out", SLOTS * SLOT)
    x, context, mask = flat(a["x"]), flat(a["ctx_1024"]), a["mask_BxS2_bk0"]
    attention(nc, "sa", False, rows_of_batch(x), None, mask, xa("sa_wq"), xa("sa_wk"), xa("sa_wv"), xa("sa_wo"),
              xa("sa_bo"), xa("ln1_g"), xa("ln1_b"), rows_of_batch(after_self))
    attention(nc, "ca", True, rows_of_batch(after_self), rows_of_batch(context), mask, xa("ca_wq"), xa("ca_wk"),
              xa("ca_wv"), xa("ca_wo"), xa("ca_bo"), xa("ln2_g"), xa("ln2_b"), rows_of_batch(after_cross))
    with (nc.sbuf_tensor("logits", [P, TT, E], F32) as logits, nc.sbuf_tensor("position", [P, TT], I32) as position,
          nc.sbuf_tensor("slot_expert", [P, SLOTS], I32) as slot_expert):
        mlp(nc, "mlp", rows_of_block(x), rows_of_block(after_cross), xa("fc1_w"), xa("fc1_b"), xa("fc2_w"), xa("fc2_b"),
            xa("ln3_g"), xa("ln3_b"), ff("w1s"), ff("w2s"), ff("w3s"), ff("Wg"), logits, rows_of_block(normed),
            rows_of_block(partial), slot_rows)
        route(nc, logits, position, slot_expert, normed, slot_rows)
        experts(nc, slot_expert, ff("W1"), ff("W2"), ff("W3"), slot_rows, slot_out)
        combine(nc, position, partial, slot_out, flat(out))


_OUTS = [((B, S, D), "float32")]


def kernel(**inputs):
    import numpy as _np
    import concourse.bacc as _bacc
    from concourse.bass_utils import run_bass_kernel_spmd as _run

    nc = _bacc.Bacc("TRN2", target_bir_lowering=False, num_devices=1)
    arrays, args = {}, {}
    for name, a in inputs.items():
        a = _np.ascontiguousarray(a)
        arrays[f"in_{name}"] = a
        args[name] = nc.dram_tensor(f"in_{name}", a.shape, mybir.dt.from_np(a.dtype), kind="ExternalInput").ap()
    outs = [nc.dram_tensor(f"out_{i}", shape, mybir.dt.from_np(_np.dtype(dt)), kind="ExternalOutput").ap()
            for i, (shape, dt) in enumerate(_OUTS)]
    build(nc, args, outs[0])
    r = _run(nc, [arrays], core_ids=[0])
    return r.results[0]["out_0"]
```
